# Optimizing a Trainium2 kernel written in Bass

```python
import numpy as np
import jax
import jax.numpy as jnp

def _softmax(x, axis=-1):
    return jax.nn.softmax(x, axis=axis)
def _gelu(x):
    return jax.nn.gelu(x, approximate=True)
def _silu(x):
    return jax.nn.silu(x)
def _sigmoid(x):
    return jax.nn.sigmoid(x)
def _layernorm(x, axis=-1, eps=1e-5):
    m = jnp.mean(x, axis=axis, keepdims=True)
    v = jnp.var(x, axis=axis, keepdims=True)
    return (x - m) / jnp.sqrt(v + eps)
def _scatter_add(tgt, idx, src, axis=0):
    return tgt.at[idx].add(src)
def _segment_sum(src, seg, n):
    return jax.ops.segment_sum(src, seg, n)

kernel_name = 'mk_adj_preln_d2_adj_512_3db684'

def setup_inputs(seed: int = 0):
    np.random.seed(seed)
    _w = jnp.asarray
    def _rec_inputs():
        import jax
        import jax.numpy as jnp
        _gk = jax.random.key(seed)
        x = -0.0005207 + 1.001 * jax.random.normal(jax.random.fold_in(_gk, 1), (4096, 512), jnp.float32)
        _w = (1.0 + jnp.arange(4096, dtype=jnp.float32)) ** -0.5
        _w = _w / _w.mean()
        _pij = jnp.clip(0.00195312 * _w[:, None] * _w[None, :], 0.0, 1.0)
        _a = jax.random.uniform(jax.random.fold_in(_gk, 2), (4096, 4096)) < _pij
        _a = jnp.logical_or(_a, jnp.eye(4096, dtype=bool))
        _af = _a.astype(jnp.float32)
        adj = _af
        return x, adj
    x, adj = _rec_inputs()
    def _L0_gnn_setup():
        import jax, jax.numpy as jnp
        import numpy as np
        N = 4096
        IN = 512
        H = 8
        D = 64
        EDGE_PROB = 0.01
        key = jax.random.key(seed)
        kx, ka, kw, ko, kd = jax.random.split(key, 5)
        x = jax.random.normal(kx, (N, IN), dtype=jnp.float32)
        adj = (jax.random.uniform(ka, (N, N)) < EDGE_PROB).astype(jnp.float32)
        adj = jnp.maximum(adj, jnp.eye(N, dtype=jnp.float32))
        W = jax.random.normal(kw, (H, IN, D), dtype=jnp.float32) * (1.0 / np.sqrt(IN))
        a_origin = jax.random.normal(ko, (H, D), dtype=jnp.float32) * 0.1
        a_dst = jax.random.normal(kd, (H, D), dtype=jnp.float32) * 0.1
        return {'x': x, 'adj': adj, 'W': W, 'a_origin': a_origin, 'a_dst': a_dst}
    _L0_gnn_all = _L0_gnn_setup()
    _L0_gnn_in = {k: v for k, v in _L0_gnn_all.items() if k in ('W', 'a_origin', 'a_dst', )}
    del _L0_gnn_all

    def _L1_gnn_setup():
        import jax, jax.numpy as jnp
        import numpy as np
        N = 4096
        INPUT_DIM = 512
        KEY_DIM = 64
        OUT_DIM = 512
        N_HEADS = 8

        def _xavier_normal(key, shape, gain):
            fan_in, fan_out = (shape[-2], shape[-1])
            std = gain * (2.0 / (fan_in + fan_out)) ** 0.5
            return jax.random.normal(key, shape, dtype=jnp.float32) * std
        key = jax.random.key(seed)
        kx, ka, kk, kq, kv, ko = jax.random.split(key, 6)
        gain = 2.0 ** 0.5
        node_matrix = jax.random.normal(kx, (N, INPUT_DIM), dtype=jnp.float32)
        adjacency_matrix = jax.random.randint(ka, (N, N), 0, 2).astype(jnp.float32)
        Wks = _xavier_normal(kk, (N_HEADS, INPUT_DIM, KEY_DIM), gain)
        Wqs = _xavier_normal(kq, (N_HEADS, INPUT_DIM, KEY_DIM), gain)
        Wvs = _xavier_normal(kv, (N_HEADS, INPUT_DIM, KEY_DIM), gain)
        Wo = _xavier_normal(ko, (N_HEADS, KEY_DIM, OUT_DIM), gain)
        return {'node_matrix': node_matrix, 'adjacency_matrix': adjacency_matrix, 'Wks': Wks, 'Wqs': Wqs, 'Wvs': Wvs, 'Wo': Wo}
    _L1_gnn_all = _L1_gnn_setup()
    _L1_gnn_in = {k: v for k, v in _L1_gnn_all.items() if k in ('Wks', 'Wqs', 'Wvs', 'Wo', )}
    del _L1_gnn_all

    return {
        "x": x,
        "adj": adj,
        "L0_gnn_W": _L0_gnn_in["W"],
        "L0_gnn_a_origin": _L0_gnn_in["a_origin"],
        "L0_gnn_a_dst": _L0_gnn_in["a_dst"],
        "L1_gnn_Wks": _L1_gnn_in["Wks"],
        "L1_gnn_Wqs": _L1_gnn_in["Wqs"],
        "L1_gnn_Wvs": _L1_gnn_in["Wvs"],
        "L1_gnn_Wo": _L1_gnn_in["Wo"],
    }

def reference(x, adj, L0_gnn_W, L0_gnn_a_origin, L0_gnn_a_dst, L1_gnn_Wks, L1_gnn_Wqs, L1_gnn_Wvs, L1_gnn_Wo):
    import jax
    import jax.numpy as jnp
    def _L0_gnn_ref(x, adj, W, a_origin, a_dst):
        import jax, jax.numpy as jnp
        import numpy as np
        N = 4096
        IN = 512
        H = 8
        D = 64
        EDGE_PROB = 0.01
        mx = jnp.einsum('nf,hfd->hnd', x, W)
        s_i = jnp.einsum('hnd,hd->hn', mx, a_origin)
        t_j = jnp.einsum('hnd,hd->hn', mx, a_dst)
        logits = s_i[:, :, None] + t_j[:, None, :]
        neg_inf = jnp.finfo(logits.dtype).min
        masked = jnp.where(adj[None] > 0, logits, neg_inf)
        attn = jax.nn.softmax(masked, axis=-1)
        out_h = jnp.einsum('hij,hjd->hid', attn, mx)
        return jnp.transpose(out_h, (1, 0, 2)).reshape(N, H * D)

    def _L1_gnn_ref(node_matrix, adjacency_matrix, Wks, Wqs, Wvs, Wo):
        import jax, jax.numpy as jnp
        import numpy as np
        N = 4096
        INPUT_DIM = 512
        KEY_DIM = 64
        OUT_DIM = 512
        N_HEADS = 8

        def _xavier_normal(key, shape, gain):
            fan_in, fan_out = (shape[-2], shape[-1])
            std = gain * (2.0 / (fan_in + fan_out)) ** 0.5
            return jax.random.normal(key, shape, dtype=jnp.float32) * std
        n = adjacency_matrix.shape[0]
        adj = jnp.maximum(adjacency_matrix, jnp.eye(n, dtype=adjacency_matrix.dtype))
        keys = jnp.einsum('nj,hjk->hnk', node_matrix, Wks)
        queries = jnp.einsum('nj,hjk->hnk', node_matrix, Wqs)
        values = jnp.einsum('nj,hjk->hnk', node_matrix, Wvs)
        key_dim = Wks.shape[-1]
        atts = jnp.einsum('hqk,hmk->hqm', queries, keys) / key_dim ** 0.5
        atts = atts - 1e+16 * (1.0 - adj)[None, :, :]
        atts = jax.nn.softmax(atts, axis=-1)
        return jnp.einsum('hqm,hmk,hko->qo', atts, values, Wo)

    h = jnp.maximum(_layernorm(x, axis=-1), 0.0)
    x = x + _L0_gnn_ref(h, adj, L0_gnn_W, L0_gnn_a_origin, L0_gnn_a_dst)
    h = jnp.maximum(_layernorm(x, axis=-1), 0.0)
    x = x + _L1_gnn_ref(h, adj, L1_gnn_Wks, L1_gnn_Wqs, L1_gnn_Wvs, L1_gnn_Wo)
    return x


_drawn_inputs = setup_inputs


def setup_inputs(seed=0):
    import zlib

    import numpy as np

    out = dict(_drawn_inputs(seed))
    spreads = {}
    factors = {}
    for name, (base, spread) in spreads.items():
        noise = np.random.default_rng([zlib.crc32(name.encode()), seed]).standard_normal(out[name].shape)
        drawn = base * np.exp(spread * noise) if base else spread * noise
        out[name] = jnp.asarray(drawn.astype(out[name].dtype))
    for name, factor in factors.items():
        out[name] = (out[name] * factor).astype(out[name].dtype)
    return out
```

```python
import concourse.bass as bass
from concourse import mybir
from contextlib import ExitStack

F32 = mybir.dt.float32
BF16 = mybir.dt.bfloat16
FP16 = mybir.dt.float16
FP8 = mybir.dt.float8e4
U8 = mybir.dt.uint8
ALU = mybir.AluOpType
ACT = mybir.ActivationFunctionType
AX = mybir.AxisListType
RMAX = bass.bass_isa.ReduceOp.max

P = 128
N = 4096
D = 512
H = 8
HD = D // H
NT = N // P
FC = D // P
PAIRS = H // 2
BLK = 512
NB = N // BLK
TB = BLK // P
CH = 4
KC = NT // CH
CW = N // CH
EPS = 1e-5
HEADROOM0 = 60.0
HEADROOM1 = 60.0
QK_TOP = 16384.0
EDGE = 2.0
SB = 3
PB = 4
SG = 8
KB = 1024


def graph_layers(nc, x, adj, w0, a_dst, wk, wq, wv, wo, out):
    ctx = ExitStack()
    with ctx:
        def sb(name, shape, dt):
            return ctx.enter_context(nc.sbuf_tensor(name, shape, dt))

        def sem(name):
            return ctx.enter_context(nc.semaphore(name))

        adjt_dram = nc.dram_tensor("adjt_dram", [NT, P, N], U8, kind="Internal").ap()
        x1_dram = nc.dram_tensor("x1_dram", [N, D], F32, kind="Internal").ap()
        q_dram = nc.dram_tensor("q_dram", [NB, 2, H, HD, BLK], FP16, kind="Internal").ap()

        nodes = sb("nodes", [P, NT, D], F32)
        wide = sb("wide", [P, 96 * KB // 4], F32)
        work = sb("work", [P, 45568 // 4], F32)

        def part(region, at, nbytes, dt):
            return region[:, at // 4:(at + nbytes) // 4].bitcast(dt)

        hta = part(wide, 0, 4 * KB, F32).rearrange("p (b c n) -> p b c n", b=2, c=FC)
        ha = part(wide, 4 * KB, 8 * KB, F32).rearrange("p (b n) -> p b n", b=TB)
        w0_sb = part(wide, 12 * KB, 8 * KB, F32).rearrange("p (c n) -> p c n", c=FC)
        adst = part(wide, 20 * KB, 2 * KB, F32)
        prod = part(wide, 22 * KB, 4 * KB, F32).rearrange("p (b n) -> p b n", b=2)
        emx = part(wide, 0, 96 * KB, BF16).rearrange("p (t s n) -> p t s n", t=NT, s=3)
        val = part(work, 16 * KB, 16 * KB, F32).rearrange("p (b t n) -> p b t n", b=2, t=TB)
        tall = part(work, 38 * KB, KB, F32).rearrange("p (t h) -> p t h", t=NT)
        expt = part(work, 39 * KB, KB, F32).rearrange("p (t h) -> p t h", t=NT)
        esplit = part(work, 40 * KB, 3 * KB // 2, BF16).rearrange("p (t s h) -> p t s h", t=NT, s=3)
        adjf = part(work, 0, 16 * KB, F32).rearrange("p (c n) -> p c n", c=CH)
        adjb = part(work, 16 * KB, 8 * KB, BF16).rearrange("p (c n) -> p c n", c=CH)
        adjt = part(work, 24 * KB, 8 * KB, FP8).rearrange("p (b n) -> p b n", b=2)
        adjt_bytes = part(work, 24 * KB, 8 * KB, U8).rearrange("p (b n) -> p b n", b=2)
        xt = part(work, 32 * KB, 4 * KB, F32).rearrange("p (b n) -> p b n", b=2)
        att0 = part(work, 36 * KB, 2 * KB, F32)
        wq_sb = part(work, 0, 8 * KB, F32).rearrange("p (c n) -> p c n", c=FC)
        wk_sb = part(work, 8 * KB, 8 * KB, F32).rearrange("p (c n) -> p c n", c=FC)
        wv_sb = part(work, 16 * KB, 8 * KB, F32).rearrange("p (c n) -> p c n", c=FC)
        wo_sb = part(work, 24 * KB, 8 * KB, F32).rearrange("p (c n) -> p c n", c=FC)
        hd = part(work, 32 * KB, 4 * KB, F32).rearrange("p (b n) -> p b n", b=2)
        keys = part(wide, 0, 64 * KB, FP16).rearrange("p (h n) -> p h n", h=H)
        htd = part(wide, 64 * KB, 16 * KB, F32).rearrange("p (b c n) -> p b c n", b=2, c=FC)
        wsq = part(wide, 80 * KB, 8 * KB, F32)
        hi = part(wide, 80 * KB, 4 * KB, FP16).rearrange("p (b n) -> p b n", b=4)
        lo = part(wide, 84 * KB, 4 * KB, FP16).rearrange("p (b n) -> p b n", b=4)
        sq = part(wide, 88 * KB, 2 * KB, BF16).rearrange("p (b n) -> p b n", b=2)
        norm_max = part(wide, 90 * KB, 4 * NB * 8, F32)
        mask = part(wide, 64 * KB, 16 * KB, U8).rearrange("p (t k n) -> p t k n", t=TB, k=NT)
        qs = part(wide, 80 * KB, 16 * KB, FP16).rearrange("p (r s h n) -> p r s h n", r=PAIRS, s=2, h=2)
        prob = part(work, 0, 16 * KB, F32).rearrange("p (b h n) -> p b h n", b=4, h=2)
        psums = part(work, 16 * KB, 8 * KB, F32).rearrange("p (b h n) -> p b h n", b=2, h=2)
        xo = part(work, 40 * KB, 4 * KB, F32).rearrange("p (b n) -> p b n", b=2)
        ot = part(work, 32 * KB, 8 * KB, F32).rearrange("p (r n) -> p r n", r=PAIRS)

        identf = sb("identf", [P, P], F32)
        identb = sb("identb", [P, P], BF16)
        headones = sb("headones", [P, P], BF16)
        onesf = sb("onesf", [P, P], F32)
        stats = sb("stats", [P, NT, 6], F32)
        mv = sb("mv", [P, NT, 2], F32)
        mv1 = sb("mv1", [P, 2, 2], F32)
        std = sb("std", [P, NT], F32)
        rstd = sb("rstd", [P, NT], F32)
        nmr = sb("nmr", [P, NT], F32)
        small = sb("small", [P, 48], F32)
        eps_c, room_c = small[:, 0:1], small[:, 1:2]
        tmax, tmax_all = small[:, 2:10], small[:, 10:18]
        den8, rden8 = small[:, 18:26], small[:, 26:34]
        wmax, wrt, wsc = small[:, 34:36], small[:, 36:38], small[:, 38:40]
        nm2, nm2_all = small[:, 40:42], small[:, 42:44]
        s_prod, s_root, alpha, neg_shift = (small[:, k:k + 1] for k in (44, 45, 46, 47))

        bank = [ctx.enter_context(nc.psum_tensor(f"bank{i}", [P, BLK], F32)) for i in range(6, 8)]
        score = [ctx.enter_context(nc.psum_tensor(f"score{i}", [P, 2, BLK], F32)) for i in range(SB)]
        bank = [sc[:, e, :] for sc in score for e in range(2)] + [b[:, :] for b in bank]

        consts_ready, waits_passed = sem("consts_ready"), sem("waits_passed")
        zeroed = sem("zeroed")
        x_in = [sem(f"x_in{g}") for g in range(NB)]
        w0_in, adst_in = sem("w0_in"), sem("adst_in")
        stats_done, aggr_done = sem("stats_done"), sem("aggr_done")
        std_done, rstd_done, nmr_done = sem("std_done"), sem("rstd_done"), sem("nmr_done")
        a_h, a_tr, a_ht, a_mm, a_mx = sem("a_h"), sem("a_tr"), sem("a_ht"), sem("a_mm"), sem("a_mx")
        a_prod, a_t = sem("a_prod"), sem("a_t")
        tmax_done, tmax_all_done = sem("tmax_done"), sem("tmax_all_done")
        tsub_done, exp_done = sem("tsub_done"), sem("exp_done")
        e_hi, e_rest2, e_low = (sem(n) for n in ("e_hi", "e_rest2", "e_low"))
        b_val, b_hi, b_rest, b_mid, b_low = (sem(n) for n in ("b_val", "b_hi", "b_rest", "b_mid", "b_low"))
        adj_in = [sem(f"adj_in{c}") for c in range(CH)]
        c_cast, c_tr, c_adjt, c_mm, c_acc = (sem(n) for n in ("c_cast", "c_tr", "c_adjt", "c_mm", "c_acc"))
        xt_in = [sem(f"xt_in{u}") for u in range(2)]
        adjt_out = [sem(f"adjt_out{u}") for u in range(2)]
        c_den, c_rden, c_att, c_x1, c_stat, c_aggr = (sem(n) for n in ("c_den", "c_rden", "c_att", "c_x1", "c_stat", "c_aggr"))
        x1_out, c_mv = sem("x1_out"), sem("c_mv")
        wq_in, wk_in, wv_in, wo_in = (sem(n) for n in ("wq_in", "wk_in", "wv_in", "wo_in"))
        d_wsq, d_wnorm, d_wmax, d_wrt, d_wsc, d_scales = (sem(n) for n in ("d_wsq", "d_wnorm", "d_wmax", "d_wrt", "d_wsc", "d_scales"))
        d_h, d_tr, d_ht, d_v, d_vout = (sem(n) for n in ("d_h", "d_tr", "d_ht", "d_v", "d_vout"))
        d_qk, d_hi, d_lo, d_sq, d_nrm, d_nmax = (sem(n) for n in ("d_qk", "d_hi", "d_lo", "d_sq", "d_nrm", "d_nmax"))
        hi_out = [sem(f"hi_out{b}") for b in range(4)]
        lo_out = [sem(f"lo_out{b}") for b in range(4)]
        d_nm2, d_nm2_all, d_sprod, d_root, d_shift = (sem(n) for n in ("d_nm2", "d_nm2_all", "d_sprod", "d_root", "d_shift"))
        q_in = [sem(f"q_in{r}") for r in range(PAIRS)]
        mask_in = [sem(f"mask_in{c}") for c in range(CH)]
        s_ready, s_exp, p_masked, pv_done, sum_done, den_done = (sem(n) for n in ("s_ready", "s_exp", "p_masked", "pv_done", "sum_done", "den_done"))
        pair_added = sem("pair_added")
        o_copied, rden_done, ot_done, wo_done, out_ready = (sem(n) for n in ("o_copied", "rden_done", "ot_done", "wo_done", "out_ready"))
        xo_in = [sem(f"xo_in{b}") for b in range(2)]
        out_stored = [sem(f"out_stored{b}") for b in range(2)]

        STEPS = PAIRS * NT
        GROUPS = STEPS // SG
        SUMS = SG - 2

        after = {12: 0, 17: 1, 22: 2, 27: 3}
        ring = []
        for k in range(STEPS):
            ring.append(("scores", k))
            if k in after:
                ring.append(("output", after[k]))
        assert len(ring) % SB == 0 and len(after) == TB

        def settled(engine):
            engine.sem_inc(waits_passed, 1)

        block = ctx.enter_context(nc.Block())

        @block.sync
        def _(sp):
            for b in range(4):
                sp.sem_inc(hi_out[b], 32)
                sp.sem_inc(lo_out[b], 32)
            for g in range(NB):
                sp.dma_start(nodes[:, g * TB:(g + 1) * TB, :],
                             x[g * BLK:(g + 1) * BLK, :].rearrange("(t p) d -> p t d", p=P)).then_inc(x_in[g], 16)
                if g == 0:
                    for c in range(FC):
                        sp.dma_start(w0_sb[:, c, :].rearrange("p (h d) -> p h d", h=H),
                                     w0[:, c * P:(c + 1) * P, :].rearrange("h p d -> p h d")).then_inc(w0_in, 16)
                    sp.dma_start(adst, a_dst.rearrange("(o h) d -> o (h d)", o=1).broadcast_to([P, D])).then_inc(adst_in, 16)

            def load_adj(n, c):
                sp.wait_ge(c_cast, CH * n + c + 1)
                settled(sp)
                sp.dma_start(adjf[:, c, :], adj[bass.ds(n * P, P), c * CW:(c + 1) * CW]).then_inc(adj_in[c], 16)

            def load_x(t, u):
                sp.wait_ge(c_x1, t + 1)
                settled(sp)
                sp.dma_start(xt[:, u, :], x[bass.ds(t * P, P), :]).then_inc(xt_in[u], 16)

            for u in range(2):
                sp.sem_inc(adjt_out[u], 16)

            def store_adjt(n, u):
                sp.wait_ge(c_adjt, CH + CH * (n + 1))
                settled(sp)
                sp.dma_start(adjt_dram[bass.ds(n, 1), :, :].rearrange("o p n -> (o p) n"), adjt_bytes[:, u, :]).then_inc(adjt_out[u], 16)

            def store_x1(t):
                sp.wait_ge(c_x1, 2 + t + 1)
                settled(sp)
                sp.dma_start(x1_dram[bass.ds(t * P, P), :],
                             nodes[:, bass.ds(t, 1), :].rearrange("p o d -> p (o d)")).then_inc(x1_out, 16)

            for c in range(CH):
                load_adj(0, c)
            for c in range(CH):
                load_adj(1, c)
            load_x(0, 0)
            store_adjt(0, 0)
            with sp.Fori(0, NT // 2 - 1) as i:
                for u in range(2):
                    t = 2 * i + u
                    load_x(t + 1, 1 - u)
                    for c in range(CH):
                        load_adj(t + 2, c)
                    store_adjt(t + 1, 1 - u)
                    store_x1(t)
            load_x(NT - 1, 1)
            store_adjt(NT - 1, 1)
            store_x1(NT - 2)
            store_x1(NT - 1)

            def load_w(dst, w, s, by_head):
                for c in range(FC):
                    src = w[:, c * P:(c + 1) * P, :].rearrange("h p d -> p h d") if by_head else \
                        w[2 * c:2 * c + 2, :, :].rearrange("h d n -> (h d) n")
                    to = dst[:, c, :].rearrange("p (h d) -> p h d", h=H) if by_head else dst[:, c, :]
                    sp.dma_start(to, src).then_inc(s, 16)

            sp.wait_ge(c_cast, CH + CH * NT)
            load_w(wq_sb, wq, wq_in, True)
            load_w(wk_sb, wk, wk_in, True)
            sp.wait_ge(c_tr, CH + CH * NT)
            load_w(wv_sb, wv, wv_in, True)
            sp.wait_ge(c_mm, 2 + NT)
            for u in range(2):
                sp.wait_ge(adjt_out[u], 16 * (NT // 2 + 1))
            load_w(wo_sb, wo, wo_in, False)

            def store_qk(g, idx):
                b, pair = idx % 4, idx % PAIRS
                for what, done, credit, stored, half in ((hi, d_hi, 0, hi_out, 0), (lo, d_lo, 2, lo_out, 1)):
                    sp.wait_ge(done, credit + g * 8 + idx + 1)
                    settled(sp)
                    for e in range(2):
                        src = what[e * HD:(e + 1) * HD, b, :]
                        if idx < PAIRS:
                            dst = keys[half * HD:(half + 1) * HD, 2 * pair + e, bass.ds(g * BLK, BLK)]
                        else:
                            dst = q_dram[bass.ds(g, 1), half, 2 * pair + e, :, :].rearrange("o d n -> (o d) n")
                        sp.dma_start(dst, src).then_inc(stored[b], 16)

            with sp.Fori(0, NB) as g:
                for idx in range(8):
                    store_qk(g, idx)
            for b in range(4):
                sp.wait_ge(hi_out[b], 32 * (2 * NB + 1))
                sp.wait_ge(lo_out[b], 32 * (2 * NB + 1))

            sp.wait_ge(d_v, 2 + NT)
            sp.wait_ge(d_nm2, 2)

            def load_q(qb, r):
                sp.wait_ge(s_ready, STEPS * qb + NT * (r + 1))
                settled(sp)
                for half in range(2):
                    for s in range(2):
                        sp.dma_start(qs[half * HD:(half + 1) * HD, r, s, :, :],
                                     q_dram[bass.ds(qb, 1), s, 2 * r:2 * r + 2, :, :].rearrange("o h d n -> (o d) h n")
                                     ).then_inc(q_in[r], 16)

            def load_mask(qb, c):
                sp.wait_ge(p_masked, STEPS * qb + STEPS - NT + KC * (c + 1))
                settled(sp)
                sp.dma_start(mask[:, :, c * KC:(c + 1) * KC, :].rearrange("p t k n -> p t (k n)"),
                             adjt_dram[bass.ds(qb * TB, TB), :, c * CW:(c + 1) * CW].rearrange("t p n -> p t n")
                             ).then_inc(mask_in[c], 16)

            def load_block(qb):
                load_q(qb, 0)
                load_q(qb, 1)
                load_q(qb, 2)
                for c in range(CH - 1):
                    load_mask(qb, c)
                load_q(qb, 3)
                load_mask(qb, CH - 1)

            def load_x1(qb, r):
                sp.wait_ge(out_stored[r % 2], 16 * (2 * qb + r // 2 + 1))
                settled(sp)
                sp.dma_start(xo[:, r % 2, :], x1_dram[bass.ds(qb * BLK + r * P, P), :]).then_inc(xo_in[r % 2], 16)

            def store_out(qb, r):
                sp.wait_ge(out_ready, TB * qb + r + 1)
                settled(sp)
                sp.dma_start(out[bass.ds(qb * BLK + r * P, P), :], xo[:, r % 2, :]).then_inc(out_stored[r % 2], 16)

            def finish_block(qb):
                load_x1(qb, 0)
                load_x1(qb, 1)
                store_out(qb, 0)
                load_x1(qb, 2)
                store_out(qb, 1)
                load_x1(qb, 3)
                store_out(qb, 2)
                store_out(qb, 3)

            for b in range(2):
                sp.sem_inc(out_stored[b], 16)
            load_block(0)
            with sp.Fori(1, NB) as qb:
                load_block(qb)
                finish_block(qb - 1)
            finish_block(NB - 1)
            for b in range(2):
                sp.wait_ge(out_stored[b], 16 * (2 * NB + 1))

        @block.gpsimd
        def _(pool):
            nc.gpsimd.memset(identf[:, :], 0.0).then_inc(zeroed, 1)
            nc.gpsimd.memset(identb[:, :], 0.0).then_inc(zeroed, 1)
            nc.gpsimd.memset(onesf[:, :], 1.0).then_inc(consts_ready, 1)
            nc.gpsimd.memset(eps_c, EPS).then_inc(consts_ready, 1)
            nc.gpsimd.memset(room_c, HEADROOM0).then_inc(consts_ready, 1)
            pool.wait_ge(zeroed, 2)
            for m in (identf, identb):
                nc.gpsimd.affine_select(out=m[:, :], in_=m[:, :], compare_op=ALU.not_equal, fill=1.0, base=0,
                                        pattern=[[-1, P]], channel_multiplier=1).then_inc(consts_ready, 1)

            pool.wait_ge(tmax_done, 1)
            nc.gpsimd.partition_all_reduce(tmax_all, tmax, P, RMAX).then_inc(tmax_all_done, 1)

            pool.sem_inc(d_sq, 4)
            with pool.Fori(0, NB) as g:
                for idx in range(8):
                    pool.wait_ge(d_hi, g * 8 + idx + 1)
                    pool.wait_ge(d_nrm, g * 8 + idx + 1)
                    nc.gpsimd.tensor_tensor(sq[:, idx % 2, :], hi[:, idx % 4, :], hi[:, idx % 4, :], ALU.mult).then_inc(d_sq, 1)
            pool.wait_ge(d_nm2, 2)
            nc.gpsimd.partition_all_reduce(nm2_all, nm2, P, RMAX).then_inc(d_nm2_all, 1)

            pool.sem_inc(sum_done, SUMS)
            with pool.Fori(0, NB) as qb:
                for k in range(STEPS):
                    b, g = k % SG, k // SG
                    if b < 2:
                        continue
                    pool.wait_ge(p_masked, STEPS * (qb + 1) + k + 1)
                    if b == 2:
                        pool.wait_ge(pair_added, GROUPS * qb + g + 1)
                    else:
                        pool.wait_ge(sum_done, SUMS * (GROUPS * qb + g + 1) + b - 2)
                    nc.gpsimd.tensor_tensor(psums[:, g % 2, :, :], psums[:, g % 2, :, :], prob[:, k % PB, :, :],
                                            ALU.add).then_inc(sum_done, 1)

        @block.scalar
        def _(act):
            act.wait_ge(consts_ready, 9)
            act.sem_inc(a_mx, 2)
            act.wait_ge(aggr_done, NT)
            nc.scalar.activation(std[:, :], mv[:, :, 1], ACT.Sqrt, bias=eps_c).then_inc(std_done, 1)
            act.wait_ge(nmr_done, 1)
            with act.Fori(0, NB) as g:
                for j in range(TB):
                    t = g * TB + j
                    act.wait_ge(a_tr, t + 1)
                    nc.scalar.activation(ha[:, j, :], nodes[:, bass.ds(t, 1), :].rearrange("p o d -> p (o d)"), ACT.Relu,
                                         bias=nmr[:, bass.ds(t, 1)], scale=rstd[:, bass.ds(t, 1)]).then_inc(a_h, 1)
                for j in range(TB):
                    t = g * TB + j
                    act.wait_ge(a_mm, 2 + t + 1)
                    settled(act)
                    nc.scalar.copy(nodes[:, bass.ds(t, 1), :].rearrange("p o d -> p (o d)"), bank[2 + j % 2]).then_inc(a_mx, 1)

            act.wait_ge(tsub_done, 1)
            nc.scalar.activation(expt, tall, ACT.Exp, bias=room_c).then_inc(exp_done, 1)
            act.wait_ge(exp_done, 1)
            nc.scalar.copy(esplit[:, :, 0, :], expt).then_inc(e_hi, 1)
            for g in range(NB + 1):
                if g < NB:
                    act.wait_ge(b_val, g + 1)
                    nc.scalar.copy(emx[:, g * TB:(g + 1) * TB, 0, :], val[:, g % 2, :, :]).then_inc(b_hi, 1)
                if g >= 1:
                    act.wait_ge(b_rest, g)
                    nc.scalar.copy(emx[:, (g - 1) * TB:g * TB, 1, :], val[:, (g - 1) % 2, :, :]).then_inc(b_mid, 1)

            act.sem_inc(c_adjt, CH)
            act.wait_ge(b_low, NB)

            def adjt_piece(n, u, c):
                act.wait_ge(c_tr, CH + CH * n + c + 1)
                settled(act)
                nc.scalar.activation(adjt[:, u, c * CW:(c + 1) * CW], bank[4 + c].bitcast(BF16), ACT.Copy,
                                     saturate=False).then_inc(c_adjt, 1)

            def adjt_tile(n, u, i):
                act.wait_ge(c_mm, n + 1)
                act.wait_ge(adjt_out[u], 16 * (i + 1))
                for c in range(CH):
                    adjt_piece(n, u, c)

            adjt_tile(0, 0, 0)
            with act.Fori(0, NT // 2 - 1) as i:
                adjt_tile(2 * i + 1, 1, i)
                adjt_tile(2 * i + 2, 0, i + 1)
            adjt_tile(NT - 1, 1, NT // 2 - 1)

            act.wait_ge(c_mv, NT)
            nc.scalar.activation(std[:, :], mv[:, :, 1], ACT.Sqrt, bias=eps_c).then_inc(std_done, 1)
            act.wait_ge(d_wmax, 2)
            nc.scalar.activation(wrt, wmax, ACT.Sqrt, scale=float(D)).then_inc(d_wrt, 1)
            act.sem_inc(d_vout, 2)

            def norm_tile(t, j):
                act.wait_ge(d_tr, t + 1)
                nc.scalar.activation(hd[:, j % 2, :], nodes[:, bass.ds(t, 1), :].rearrange("p o d -> p (o d)"), ACT.Relu,
                                     bias=nmr[:, bass.ds(t, 1)], scale=rstd[:, bass.ds(t, 1)]).then_inc(d_h, 1)

            act.wait_ge(nmr_done, 2)
            act.wait_ge(x1_out, 16 * NT)
            for j in range(TB):
                norm_tile(j, j)
            act.wait_ge(d_scales, 1)

            def project(g, last):
                for j in range(TB):
                    t = g * TB + j
                    if not last:
                        norm_tile(t + TB, j)
                    act.wait_ge(d_v, 2 + t + 1)
                    settled(act)
                    nc.scalar.copy(nodes[:, bass.ds(t, 1), :].rearrange("p o d -> p (o d)"), bank[2 + j % 2]).then_inc(d_vout, 1)
                for idx in range(8):
                    act.wait_ge(d_qk, 2 + g * 8 + idx + 1)
                    act.wait_ge(hi_out[idx % 4], 32 * (2 * g + idx // 4 + 1))
                    act.wait_ge(d_sq, g * 8 + idx + 1)
                    kind = 1 if idx < PAIRS else 0
                    nc.scalar.activation(hi[:, idx % 4, :], bank[4 + idx % 2], ACT.Copy,
                                         scale=wsc[:, kind:kind + 1]).then_inc(d_hi, 1)

            with act.Fori(0, NB - 1) as g:
                project(g, False)
            project(NB - 1, True)
            act.wait_ge(d_sprod, 1)
            nc.scalar.activation(s_root, s_prod, ACT.Sqrt).then_inc(d_root, 1)

            act.wait_ge(d_shift, 1)
            act.sem_inc(o_copied, 1)

            def copy_attention(qb, r):
                if r == 0:
                    act.wait_ge(wo_done, TB * qb)
                act.wait_ge(pv_done, PB + STEPS * qb + (r + 1) * NT)
                nc.scalar.copy(ot[:, r, :], bank[6]).then_inc(o_copied, 1)

            def exps(qb, first):
                for at, (kind, k) in enumerate(ring):
                    if kind == "output":
                        continue
                    act.wait_ge(s_ready, STEPS * (qb + 1) + k + 1)
                    sc = score[at % SB][:, :, :]
                    nc.scalar.activation(sc, sc, ACT.Exp, bias=neg_shift, scale=alpha).then_inc(s_exp, 1)
                    if k % NT == 1 and k > NT:
                        if k // NT == 1 and first:
                            act.wait_ge(pv_done, PB + NT)
                            nc.scalar.copy(ot[:, 0, :], bank[6]).then_inc(o_copied, 1)
                        else:
                            copy_attention(qb, k // NT - 1)
                    elif k == 1 and not first:
                        copy_attention(qb - 1, PAIRS - 1)

            exps(0, True)
            with act.Fori(1, NB) as qb:
                exps(qb, False)
            copy_attention(NB - 1, PAIRS - 1)

        @block.vector
        def _(dve):
            for e in range(2):
                for f in range(2):
                    nc.vector.memset(headones[e * HD:(e + 1) * HD, f * HD:(f + 1) * HD], float(e == f)).then_inc(consts_ready, 1)
            dve.sem_inc(a_ht, 2)
            dve.sem_inc(c_cast, CH)
            dve.sem_inc(c_acc, 2)
            dve.sem_inc(c_x1, 2)
            for g in range(NB):
                dve.wait_ge(x_in[g], 16)
                for t in range(g * TB, (g + 1) * TB):
                    nc.vector.bn_stats(stats[:, t, :], nodes[:, t, :]).then_inc(stats_done, 1)
            for t in range(NT):
                dve.wait_ge(stats_done, t + 1)
                nc.vector.bn_aggr(mv[:, t, :], stats[:, t, :]).then_inc(aggr_done, 1)

            def norm_factors(n):
                dve.wait_ge(std_done, n)
                nc.vector.reciprocal(rstd[:, :], std[:, :]).then_inc(rstd_done, 1)
                dve.wait_ge(rstd_done, n)
                nc.vector.scalar_tensor_tensor(out=nmr[:, :], in0=mv[:, :, 0], scalar=-1.0, in1=rstd[:, :],
                                               op0=ALU.mult, op1=ALU.mult).then_inc(nmr_done, 1)

            norm_factors(1)
            dve.wait_ge(adst_in, 16)
            with dve.Fori(0, NB) as g:
                for j in range(TB):
                    t = g * TB + j
                    dve.wait_ge(a_tr, TB + t + 1)
                    dve.wait_ge(a_mm, t + 1)
                    nc.vector.tensor_copy(hta[:, j % 2, :, :], bank[j % 2].rearrange("p (c n) -> p c n", c=FC)).then_inc(a_ht, 1)
                for j in range(TB):
                    t = g * TB + j
                    dve.wait_ge(a_mx, 2 + t + 1)
                    nc.vector.tensor_tensor(prod[:, j % 2, :], nodes[:, bass.ds(t, 1), :].rearrange("p o d -> p (o d)"),
                                            adst, ALU.mult).then_inc(a_prod, 1)
                    dve.wait_ge(a_prod, t + 1)
                    nc.vector.tensor_reduce(tall[:, bass.ds(t, 1), :].rearrange("p o h -> p (o h)"),
                                            prod[:, j % 2, :].rearrange("p (h d) -> p h d", h=H), AX.X, ALU.add).then_inc(a_t, 1)

            dve.wait_ge(a_t, NT)
            nc.vector.tensor_reduce(tmax, tall.rearrange("p t h -> p h t"), AX.X, ALU.max).then_inc(tmax_done, 1)
            dve.wait_ge(tmax_all_done, 1)
            nc.vector.tensor_tensor(tall, tall, tmax_all.rearrange("p (o h) -> p o h", o=1).broadcast_to([P, NT, H]),
                                    ALU.subtract).then_inc(tsub_done, 1)
            dve.wait_ge(exp_done, 1)
            for g in range(NB + 1):
                if g < NB:
                    if g >= 2:
                        dve.wait_ge(b_low, g - 1)
                    v = val[:, g % 2, :, :].rearrange("p t (h d) -> p (t h) d", h=H)
                    nc.vector.tensor_tensor(
                        v, nodes[:, g * TB:(g + 1) * TB, :].rearrange("p t (h d) -> p (t h) d", h=H),
                        expt[:, g * TB:(g + 1) * TB, :].rearrange("p t (h o) -> p (t h) o", o=1).broadcast_to([P, TB * H, HD]),
                        ALU.mult).then_inc(b_val, 1)
                    dve.wait_ge(b_hi, g + 1)
                    nc.vector.tensor_tensor(val[:, g % 2, :, :], val[:, g % 2, :, :], emx[:, g * TB:(g + 1) * TB, 0, :],
                                            ALU.subtract).then_inc(b_rest, 1)
                if g >= 1:
                    dve.wait_ge(b_mid, g)
                    nc.vector.tensor_tensor(emx[:, (g - 1) * TB:g * TB, 2, :], val[:, (g - 1) % 2, :, :],
                                            emx[:, (g - 1) * TB:g * TB, 1, :], ALU.subtract).then_inc(b_low, 1)
            dve.wait_ge(e_hi, 1)
            dve.wait_ge(b_val, NB)
            nc.vector.tensor_tensor(expt, expt, esplit[:, :, 0, :], ALU.subtract).then_inc(e_rest2, 1)
            dve.wait_ge(e_rest2, 1)
            nc.vector.tensor_copy(esplit[:, :, 1, :], expt).then_inc(e_rest2, 1)
            dve.wait_ge(e_rest2, 2)
            nc.vector.tensor_tensor(esplit[:, :, 2, :], expt, esplit[:, :, 1, :], ALU.subtract).then_inc(e_low, 1)


            def cast_tile(n, i):
                for c in range(CH):
                    dve.wait_ge(adj_in[c], 16 * (n + 1))
                    dve.wait_ge(c_tr, CH * n + c + 1)
                    nc.vector.tensor_scalar(adjb[:, c, :], adjf[:, c, :], 0.0, EDGE, ALU.is_gt, ALU.mult).then_inc(c_cast, 1)

            def finish_tile(t, u, i):
                dve.wait_ge(c_mm, 2 + t + 1)
                nc.vector.tensor_reduce(den8, bank[2 + u][:, 0:3 * H].rearrange("p (s h) -> p h s", s=3), AX.X, ALU.add).then_inc(c_den, 1)
                dve.wait_ge(c_den, t + 1)
                nc.vector.reciprocal(rden8, den8).then_inc(c_rden, 1)
                dve.wait_ge(c_rden, t + 1)
                nc.vector.tensor_tensor(att0.rearrange("p (h d) -> p h d", h=H), bank[u].rearrange("p (h d) -> p h d", h=H),
                                        rden8.rearrange("p (h o) -> p h o", o=1).broadcast_to([P, H, HD]),
                                        ALU.mult).then_inc(c_acc, 1)
                dve.wait_ge(c_acc, 2 + t + 1)
                dve.wait_ge(xt_in[u], 16 * (i + 1))
                row = nodes[:, bass.ds(t, 1), :].rearrange("p o d -> p (o d)")
                nc.vector.tensor_tensor(row, att0, xt[:, u, :], ALU.add).then_inc(c_x1, 1)
                dve.wait_ge(c_x1, 2 + t + 1)
                settled(dve)
                nc.vector.bn_stats(stats[:, u, :], row).then_inc(c_stat, 1)
                dve.wait_ge(c_stat, t + 1)
                settled(dve)
                nc.vector.bn_aggr(mv1[:, u, :], stats[:, u, :]).then_inc(c_aggr, 1)
                dve.wait_ge(c_aggr, t + 1)
                nc.vector.tensor_copy(mv[:, bass.ds(t, 1), :].rearrange("p o d -> p (o d)"), mv1[:, u, :]).then_inc(c_mv, 1)

            cast_tile(0, 0)
            with dve.Fori(0, NT // 2 - 1) as i:
                for u in range(2):
                    cast_tile(2 * i + u + 1, i)
                    finish_tile(2 * i + u, u, i)
            cast_tile(NT - 1, NT // 2 - 1)
            for u in range(2):
                finish_tile(NT - 2 + u, u, NT // 2 - 1)

            for n, (w, s) in enumerate(((wq_sb, wq_in), (wk_sb, wk_in))):
                dve.wait_ge(s, 16 * FC)
                if n == 1:
                    dve.wait_ge(d_wnorm, 1)
                dve.wait_ge(c_mm, 2 + NT)
                nc.vector.tensor_tensor(wsq, w.rearrange("p c n -> p (c n)"), w.rearrange("p c n -> p (c n)"), ALU.mult).then_inc(d_wsq, 1)
                dve.wait_ge(d_wnorm, n + 1)
                nc.vector.tensor_reduce(wmax[:, n:n + 1], bank[6 + n], AX.X, ALU.max).then_inc(d_wsc, 1)
            dve.wait_ge(d_wsc, 2)
            nc.vector.tensor_scalar(wmax, wmax, 1e-24, None, ALU.max).then_inc(d_wmax, 2)
            norm_factors(2)
            dve.wait_ge(d_wrt, 1)
            nc.vector.reciprocal(wsc, wrt).then_inc(d_wsc, 1)
            dve.wait_ge(d_wsc, 3)
            nc.vector.tensor_scalar(wsc, wsc, QK_TOP, None, ALU.mult).then_inc(d_scales, 1)
            dve.sem_inc(d_ht, 2)
            dve.sem_inc(d_lo, 2)
            dve.sem_inc(d_nmax, 2)

            def copy_ht(g, j, u):
                t = g * TB + j
                dve.wait_ge(d_tr, 2 + t + 1)
                nc.vector.tensor_copy(htd[:, u, :, j * P:(j + 1) * P], bank[j % 2].rearrange("p (c n) -> p c n", c=FC)).then_inc(d_ht, 1)

            dve.wait_ge(d_scales, 1)
            for j in range(TB):
                copy_ht(0, j, 0)

            def norms(g, idx):
                kind = 1 if idx < PAIRS else 0
                dve.wait_ge(d_nrm, 2 + g * 8 + idx + 1)
                nc.vector.tensor_reduce(norm_max[:, bass.ds(g * 8 + kind * PAIRS + idx % PAIRS, 1)],
                                        bank[6 + idx % 2], AX.X, ALU.max).then_inc(d_nmax, 1)

            def project(g, u, last):
                if not last:
                    for j in range(TB):
                        copy_ht(g + 1, j, 1 - u)
                for idx in range(8):
                    kind = 1 if idx < PAIRS else 0
                    dve.wait_ge(d_hi, g * 8 + idx + 1)
                    dve.wait_ge(lo_out[idx % 4], 32 * (2 * g + idx // 4 + 1))
                    nc.vector.scalar_tensor_tensor(out=lo[:, idx % 4, :], in0=bank[4 + idx % 2], scalar=wsc[:, kind:kind + 1],
                                                   in1=hi[:, idx % 4, :], op0=ALU.mult, op1=ALU.subtract).then_inc(d_lo, 1)
                    if idx >= 2:
                        norms(g, idx - 2)
                norms(g, 6)
                norms(g, 7)

            with dve.Fori(0, NB // 2 - 1) as i:
                project(2 * i, 0, False)
                project(2 * i + 1, 1, False)
            project(NB - 2, 0, False)
            project(NB - 1, 1, True)

            dve.wait_ge(d_nmax, 2 + 8 * NB)
            for kind in range(2):
                nc.vector.tensor_reduce(nm2[:, kind:kind + 1],
                                        norm_max.rearrange("p (g k r) -> p k g r", g=NB, k=2)[:, kind, :, :],
                                        AX.XY, ALU.max).then_inc(d_nm2, 1)
            dve.wait_ge(d_nm2_all, 1)
            nc.vector.tensor_tensor(s_prod, nm2_all[:, 0:1], nm2_all[:, 1:2], ALU.mult).then_inc(d_sprod, 1)
            nc.vector.tensor_tensor(alpha, wrt[:, 0:1], wrt[:, 1:2], ALU.mult).then_inc(d_wsc, 1)
            dve.wait_ge(d_wsc, 4)
            nc.vector.tensor_scalar(alpha, alpha, 1.0 / (HD ** 0.5 * QK_TOP * QK_TOP), None, ALU.mult).then_inc(d_wsc, 1)
            dve.wait_ge(d_wsc, 5)
            dve.wait_ge(d_root, 1)
            nc.vector.scalar_tensor_tensor(out=neg_shift, in0=s_root, scalar=-1.0, in1=alpha, op0=ALU.mult, op1=ALU.mult).then_inc(d_wsc, 1)
            dve.wait_ge(d_wsc, 6)
            nc.vector.tensor_scalar(neg_shift, neg_shift, HEADROOM1, 0.0, ALU.add, ALU.min).then_inc(d_shift, 1)

            dve.sem_inc(p_masked, STEPS)
            dve.sem_inc(ot_done, 1)

            def finish_pair(qb, r):
                dve.wait_ge(den_done, 2 + GROUPS * qb + (r + 1) * NT // SG)
                nc.vector.reciprocal(bank[7], bank[7]).then_inc(rden_done, 1)
                dve.wait_ge(rden_done, PAIRS * qb + r + 1)
                dve.wait_ge(o_copied, 1 + PAIRS * qb + r + 1)
                nc.vector.tensor_tensor(ot[:, r, :], ot[:, r, :], bank[7], ALU.mult).then_inc(ot_done, 1)

            def add_x1(qb, r, src):
                dve.wait_ge(wo_done, TB * qb + r + 1)
                dve.wait_ge(xo_in[r % 2], 16 * (2 * qb + r // 2 + 1))
                nc.vector.tensor_tensor(xo[:, r % 2, :], xo[:, r % 2, :], src, ALU.add).then_inc(out_ready, 1)

            def masks(qb, first):
                for at, (kind, k) in enumerate(ring):
                    if kind == "output":
                        if not first:
                            add_x1(qb - 1, k, score[at % SB][:, 0, :])
                        continue
                    r, kt = k // NT, k % NT
                    if r == 0 and kt % KC == 0:
                        dve.wait_ge(mask_in[kt // KC], 16 * (qb + 1))
                    dve.wait_ge(s_exp, STEPS * qb + k + 1)
                    dve.wait_ge(pv_done, STEPS * qb + k + 1)
                    g, b = (k - PB) // SG, (k - PB) % SG
                    if b < 2:
                        dve.wait_ge(pair_added, GROUPS * qb + g + 1)
                    else:
                        dve.wait_ge(sum_done, SUMS * (GROUPS * qb + g + 1) + b - 1)
                    nc.vector.tensor_tensor(prob[:, k % PB, :, :].rearrange("p h (t n) -> p h t n", t=TB),
                                            score[at % SB][:, :, :].rearrange("p h (t n) -> p h t n", t=TB),
                                            mask[:, :, kt, :].unsqueeze(1).broadcast_to([P, 2, TB, P]), ALU.mult).then_inc(p_masked, 1)
                    if k % SG == 1:
                        g = k // SG
                        dve.wait_ge(p_masked, STEPS * (qb + 1) + k + 1)
                        dve.wait_ge(den_done, GROUPS * qb + g + 1)
                        nc.vector.tensor_tensor(psums[:, g % 2, :, :], prob[:, (k - 1) % PB, :, :], prob[:, k % PB, :, :],
                                                ALU.add).then_inc(pair_added, 1)
                    if kt == 5:
                        if r:
                            finish_pair(qb, r - 1)
                        elif not first:
                            finish_pair(qb - 1, PAIRS - 1)

            masks(0, True)
            with dve.Fori(1, NB) as qb:
                masks(qb, False)
            finish_pair(NB - 1, PAIRS - 1)
            for r in range(TB):
                add_x1(NB - 1, r, score[r % SB][:, 0, :])

        @block.tensor
        def _(pe):
            pe.wait_ge(consts_ready, 9)
            pe.sem_inc(a_tr, TB)
            pe.sem_inc(a_mm, 2)
            pe.sem_inc(c_tr, CH)
            pe.sem_inc(c_mm, 2)
            pe.sem_inc(d_tr, 2)
            pe.sem_inc(d_v, 2)
            pe.sem_inc(d_qk, 2)
            pe.sem_inc(d_nrm, 2)
            pe.wait_ge(w0_in, 16 * FC)
            with pe.Fori(0, NB) as g:
                def transpose_a(j):
                    t = g * TB + j
                    pe.wait_ge(a_h, t + 1)
                    pe.wait_ge(a_ht, t + 1)
                    for c in range(FC):
                        last = nc.tensor.transpose(bank[j % 2][:, c * P:(c + 1) * P], ha[:, j, c * P:(c + 1) * P], identf[:, :])
                    last.then_inc(a_tr, 1)

                def project_a(j):
                    t = g * TB + j
                    pe.wait_ge(a_ht, 2 + t + 1)
                    pe.wait_ge(a_mx, t + 1)
                    for c in range(FC):
                        last = nc.tensor.matmul(bank[2 + j % 2], hta[:, j % 2, c, :], w0_sb[:, c, :], start=c == 0, stop=c == FC - 1)
                    last.then_inc(a_mm, 1)

                transpose_a(0)
                for j in range(TB):
                    if j + 1 < TB:
                        transpose_a(j + 1)
                    project_a(j)

            def transpose_adj(n, c):
                pe.wait_ge(c_cast, CH + CH * n + c + 1)
                pe.wait_ge(c_adjt, CH * n + c + 1)
                for k in range(KC):
                    last = nc.tensor.transpose(bank[4 + c].bitcast(BF16)[:, k * P:(k + 1) * P], adjb[:, c, k * P:(k + 1) * P], identb[:, :])
                last.then_inc(c_tr, 1)

            for c in range(CH):
                transpose_adj(0, c)
            pe.wait_ge(b_low, NB)
            pe.wait_ge(e_low, 1)

            def attend(t, u, last_tile):
                pe.wait_ge(c_acc, t + 1)
                for c in range(CH):
                    pe.wait_ge(c_adjt, CH + CH * t + c + 1)
                    settled(pe)
                    for k in range(c * KC, (c + 1) * KC):
                        first, last_k = k == 0, k == NT - 1
                        w = adjt[:, u, k * P:(k + 1) * P]
                        for s in range(3):
                            nc.tensor.matmul(bank[u], w, emx[:, k, s, :], start=first and s == 0, stop=last_k and s == 2)
                        last = nc.tensor.matmul(bank[2 + u][:, 0:3 * H], w, esplit[:, k, :, :].rearrange("p s h -> p (s h)"),
                                                start=first, stop=last_k)
                    if c == CH - 1:
                        last.then_inc(c_mm, 1)
                    if not last_tile:
                        transpose_adj(t + 1, c)

            with pe.Fori(0, NT // 2 - 1) as i:
                for u in range(2):
                    attend(2 * i + u, u, False)
            attend(NT - 2, 0, False)
            attend(NT - 1, 1, True)

            for n in range(2):
                pe.wait_ge(d_wsq, n + 1)
                for c in range(FC):
                    last = nc.tensor.matmul(bank[6 + n], onesf[:, :], wsq[:, c * D:(c + 1) * D], start=c == 0, stop=c == FC - 1)
                last.then_inc(d_wnorm, 1)

            def transpose_d(g, j):
                t = g * TB + j
                pe.wait_ge(d_h, t + 1)
                pe.wait_ge(d_ht, t + 1)
                for c in range(FC):
                    last = nc.tensor.transpose(bank[j % 2][:, c * P:(c + 1) * P], hd[:, j % 2, c * P:(c + 1) * P], identf[:, :])
                last.then_inc(d_tr, 1)

            def project(g, u, last_block):
                pe.wait_ge(d_ht, 2 + TB * (g + 1))
                for j in range(TB):
                    t = g * TB + j
                    pe.wait_ge(d_vout, t + 1)
                    for c in range(FC):
                        last = nc.tensor.matmul(bank[2 + j % 2], htd[:, u, c, j * P:(j + 1) * P], wv_sb[:, c, :], start=c == 0, stop=c == FC - 1)
                    last.then_inc(d_v, 1)
                    if not last_block:
                        transpose_d(g + 1, j)

                def norm(idx):
                    pe.wait_ge(d_sq, 4 + g * 8 + idx + 1)
                    pe.wait_ge(d_nmax, g * 8 + idx + 1)
                    nc.tensor.matmul(bank[6 + idx % 2], headones[:, :], sq[:, idx % 2, :], start=True, stop=True).then_inc(d_nrm, 1)

                for idx in range(8):
                    w = wk_sb if idx < PAIRS else wq_sb
                    pair = idx % PAIRS
                    pe.wait_ge(d_lo, g * 8 + idx + 1)
                    for c in range(FC):
                        last = nc.tensor.matmul(bank[4 + idx % 2], w[:, c, pair * P:(pair + 1) * P], htd[:, u, c, :], start=c == 0, stop=c == FC - 1)
                    last.then_inc(d_qk, 1)
                    if idx >= 2:
                        norm(idx - 2)
                norm(6)
                norm(7)

            for j in range(TB):
                transpose_d(0, j)
            pe.wait_ge(wv_in, 16 * FC)
            with pe.Fori(0, NB // 2 - 1) as i:
                project(2 * i, 0, False)
                project(2 * i + 1, 1, False)
            project(NB - 2, 0, False)
            project(NB - 1, 1, True)

            pe.sem_inc(s_ready, STEPS)
            pe.sem_inc(pv_done, PB)
            pe.sem_inc(den_done, 2)
            pe.wait_ge(d_vout, 2 + NT)
            pe.wait_ge(d_shift, 1)
            pe.wait_ge(wo_in, 16 * FC)

            def scores(qb, k, buf):
                r, kt = k // NT, k % NT
                if kt == 0:
                    pe.wait_ge(q_in[r], 64 * (qb + 1))
                for e in range(2):
                    for s in range(2):
                        last = nc.tensor.matmul(score[buf][:, e, :], keys[:, 2 * r + e, kt * P:(kt + 1) * P],
                                                qs[:, r, s, e, :], start=s == 0, stop=s == 1)
                last.then_inc(s_ready, 1)

            def output(qb, r, buf):
                pe.wait_ge(ot_done, 1 + PAIRS * (qb + 1))
                for c in range(PAIRS):
                    last = nc.tensor.matmul(score[buf][:, 0, :], ot[:, c, r * P:(r + 1) * P], wo_sb[:, c, :],
                                            start=c == 0, stop=c == PAIRS - 1)
                last.then_inc(wo_done, 1)

            def values(qb, k):
                r, kt = k // NT, k % NT
                if kt == 0:
                    pe.wait_ge(o_copied, PAIRS * qb + r + 1)
                pe.wait_ge(p_masked, STEPS * (qb + 1) + k + 1)
                for e in range(2):
                    last = nc.tensor.matmul(bank[6][e * HD:(e + 1) * HD, :],
                                            nodes[:, kt, (2 * r + e) * HD:(2 * r + e + 1) * HD],
                                            prob[:, k % PB, e, :], start=kt == 0, stop=kt == NT - 1)
                last.then_inc(pv_done, 1)

            def denominators(qb, g):
                r, first, last_group = g // (NT // SG), g % (NT // SG) == 0, (g + 1) % (NT // SG) == 0
                if first:
                    pe.wait_ge(ot_done, PAIRS * qb + r + 1)
                pe.wait_ge(sum_done, SUMS * (GROUPS * qb + g + 2))
                for e in range(2):
                    last = nc.tensor.matmul(bank[7][e * HD:(e + 1) * HD, :], onesf[:, 0:HD], psums[:, g % 2, e, :],
                                            start=first, stop=last_group)
                last.then_inc(den_done, 1)

            def attention(qb, first):
                for at in range(len(ring)):
                    before, k = ring[at - SB]
                    if at < SB:
                        if not first:
                            values(qb - 1, k)
                    elif before == "scores":
                        values(qb, k)
                        if k % SG == 2 and k > SG:
                            denominators(qb, k // SG - 1)
                        elif k == 2 and not first:
                            denominators(qb - 1, GROUPS - 1)
                    elif not first:
                        pe.wait_ge(out_ready, TB * (qb - 1) + k + 1)
                    kind, k = ring[at]
                    if kind == "scores":
                        scores(qb, k, at % SB)
                    elif not first:
                        output(qb - 1, k, at % SB)

            attention(0, True)
            with pe.Fori(1, NB) as qb:
                attention(qb, False)
            for at in range(-SB, 0):
                values(NB - 1, ring[at][1])
            denominators(NB - 1, GROUPS - 1)
            for r in range(TB):
                if r >= SB:
                    pe.wait_ge(out_ready, TB * (NB - 1) + r - SB + 1)
                output(NB - 1, r, r % SB)


_INS = ["x", "adj", "L0_gnn_W", "L0_gnn_a_dst", "L1_gnn_Wks", "L1_gnn_Wqs", "L1_gnn_Wvs", "L1_gnn_Wo"]


def kernel(x, adj, L0_gnn_W, L0_gnn_a_origin, L0_gnn_a_dst, L1_gnn_Wks, L1_gnn_Wqs, L1_gnn_Wvs, L1_gnn_Wo):
    import numpy as _np
    import concourse.bacc as _bacc
    from concourse import mybir as _mybir
    from concourse.bass_utils import run_bass_kernel_spmd as _run

    given = dict(zip(_INS, (x, adj, L0_gnn_W, L0_gnn_a_dst, L1_gnn_Wks, L1_gnn_Wqs, L1_gnn_Wvs, L1_gnn_Wo)))
    nc = _bacc.Bacc("TRN2", target_bir_lowering=False, num_devices=1)
    arrays, args = {}, []
    for name in _INS:
        a = _np.ascontiguousarray(given[name])
        arrays[f"in_{name}_dram"] = a
        args.append(nc.dram_tensor(f"in_{name}_dram", a.shape, _mybir.dt.from_np(a.dtype), kind="ExternalInput").ap())
    out = nc.dram_tensor("out_0_dram", (N, D), F32, kind="ExternalOutput").ap()
    graph_layers(nc, *args, out)
    r = _run(nc, [arrays], core_ids=[0])
    return r.results[0]["out_0_dram"]
```

```python
import concourse.bass as bass
from concourse import mybir
from contextlib import ExitStack

F32 = mybir.dt.float32
BF16 = mybir.dt.bfloat16
FP16 = mybir.dt.float16
FP8 = mybir.dt.float8e4
U8 = mybir.dt.uint8
ALU = mybir.AluOpType
ACT = mybir.ActivationFunctionType
AX = mybir.AxisListType
RMAX = bass.bass_isa.ReduceOp.max

P = 128
N = 4096
D = 512
H = 8
HD = D // H
NT = N // P
FC = D // P
PAIRS = H // 2
BLK = 512
NB = N // BLK
TB = BLK // P
CH = 4
KC = NT // CH
CW = N // CH
EPS = 1e-5
HEADROOM0 = 60.0
NARROW = 9.0
MX_TOP = 32768.0
E_TOP = 16384.0
HEADROOM1 = 60.0
QK_TOP = 16384.0
EDGE = 2.0
SB = 3
PB = 4
SG = 8
KB = 1024


def graph_layers(nc, x, adj, w0, a_dst, wk, wq, wv, wo, out):
    ctx = ExitStack()
    with ctx:
        def sb(name, shape, dt):
            return ctx.enter_context(nc.sbuf_tensor(name, shape, dt))

        def sem(name):
            return ctx.enter_context(nc.semaphore(name))

        adjt_dram = nc.dram_tensor("adjt_dram", [NT, P, N], U8, kind="Internal").ap()
        x1_dram = nc.dram_tensor("x1_dram", [N, D], F32, kind="Internal").ap()
        q_dram = nc.dram_tensor("q_dram", [NB, 2, H, HD, BLK], FP16, kind="Internal").ap()

        nodes = sb("nodes", [P, NT, D], F32)
        wide = sb("wide", [P, 96 * KB // 4], F32)
        work = sb("work", [P, 45568 // 4], F32)

        def part(region, at, nbytes, dt):
            return region[:, at // 4:(at + nbytes) // 4].bitcast(dt)

        hta = part(wide, 0, 4 * KB, F32).rearrange("p (b c n) -> p b c n", b=2, c=FC)
        ha = part(wide, 4 * KB, 8 * KB, F32).rearrange("p (b n) -> p b n", b=TB)
        w0_sb = part(wide, 12 * KB, 8 * KB, F32).rearrange("p (c n) -> p c n", c=FC)
        adst = part(wide, 20 * KB, 2 * KB, F32)
        prod = part(wide, 22 * KB, 4 * KB, F32).rearrange("p (b n) -> p b n", b=2)
        emx = part(wide, 0, 96 * KB, BF16).rearrange("p (t s n) -> p t s n", t=NT, s=3)
        emx_pair = part(wide, 0, 96 * KB, FP16).rearrange("p (t s n) -> p t s n", t=NT, s=3)
        tall = part(work, 38 * KB, KB, F32).rearrange("p (t h) -> p t h", t=NT)
        expt = part(work, 39 * KB, KB, F32).rearrange("p (t h) -> p t h", t=NT)
        esplit = part(work, 40 * KB, 3 * KB // 2, BF16).rearrange("p (t s h) -> p t s h", t=NT, s=3)
        esplit_pair = part(work, 40 * KB, 3 * KB // 2, FP16).rearrange("p (t s h) -> p t s h", t=NT, s=3)
        erest = part(work, 42 * KB, KB, F32).rearrange("p (t h) -> p t h", t=NT)
        adjf = part(work, 0, 16 * KB, F32).rearrange("p (c n) -> p c n", c=CH)
        adjb = part(work, 16 * KB, 8 * KB, BF16).rearrange("p (c n) -> p c n", c=CH)
        adjt = part(work, 24 * KB, 8 * KB, FP8).rearrange("p (b n) -> p b n", b=2)
        adjt_bytes = part(work, 24 * KB, 8 * KB, U8).rearrange("p (b n) -> p b n", b=2)
        xt = part(work, 32 * KB, 4 * KB, F32).rearrange("p (b n) -> p b n", b=2)
        att0 = part(work, 36 * KB, 2 * KB, F32)
        wq_sb = part(work, 0, 8 * KB, F32).rearrange("p (c n) -> p c n", c=FC)
        wk_sb = part(work, 8 * KB, 8 * KB, F32).rearrange("p (c n) -> p c n", c=FC)
        wv_sb = part(work, 16 * KB, 8 * KB, F32).rearrange("p (c n) -> p c n", c=FC)
        wo_sb = part(work, 24 * KB, 8 * KB, F32).rearrange("p (c n) -> p c n", c=FC)
        hd = part(work, 32 * KB, 4 * KB, F32).rearrange("p (b n) -> p b n", b=2)
        keys = part(wide, 0, 64 * KB, FP16).rearrange("p (h n) -> p h n", h=H)
        htd = part(wide, 64 * KB, 16 * KB, F32).rearrange("p (b c n) -> p b c n", b=2, c=FC)
        wsq = part(wide, 80 * KB, 8 * KB, F32)
        hi = part(wide, 80 * KB, 4 * KB, FP16).rearrange("p (b n) -> p b n", b=4)
        lo = part(wide, 84 * KB, 4 * KB, FP16).rearrange("p (b n) -> p b n", b=4)
        sq = part(wide, 88 * KB, 2 * KB, BF16).rearrange("p (b n) -> p b n", b=2)
        norm_max = part(wide, 90 * KB, 4 * NB * 8, F32)
        mask = part(wide, 64 * KB, 16 * KB, U8).rearrange("p (t k n) -> p t k n", t=TB, k=NT)
        qs = part(wide, 80 * KB, 16 * KB, FP16).rearrange("p (r s h n) -> p r s h n", r=PAIRS, s=2, h=2)
        prob = part(work, 0, 16 * KB, F32).rearrange("p (b h n) -> p b h n", b=4, h=2)
        psums = part(work, 16 * KB, 8 * KB, F32).rearrange("p (b h n) -> p b h n", b=2, h=2)
        xo = part(work, 40 * KB, 4 * KB, F32).rearrange("p (b n) -> p b n", b=2)
        ot = part(work, 32 * KB, 8 * KB, F32).rearrange("p (r n) -> p r n", r=PAIRS)

        identf = sb("identf", [P, P], F32)
        identb = sb("identb", [P, P], BF16)
        headones = sb("headones", [P, P], BF16)
        onesf = sb("onesf", [P, P], F32)
        stats = sb("stats", [P, TB, 6], F32)
        mv = sb("mv", [P, NT, 2], F32)
        mv1 = sb("mv1", [P, 2, 2], F32)
        mva = sb("mva", [P, TB, 2], F32)
        std = sb("std", [P, NT], F32)
        rstd = sb("rstd", [P, NT], F32)
        nmr = sb("nmr", [P, NT], F32)
        small = sb("small", [P, 48], F32)
        ext = sb("ext", [P, 2 * H + 1], F32)
        ext_all = sb("ext_all", [P, 2 * H + 1], F32)
        mabs = sb("mabs", [P, NT], F32)
        wide_range = sb("wide_range", [P, 1], mybir.dt.int32)
        eps_c, room_c = small[:, 0:1], small[:, 1:2]
        mx_scale, mx_over, t_range = small[:, 2:3], small[:, 3:4], small[:, 4:5]
        range8 = small[:, 10:18]
        den8, rden8 = small[:, 18:26], small[:, 26:34]
        wmax, wrt, wsc = small[:, 34:36], small[:, 36:38], small[:, 38:40]
        nm2, nm2_all = small[:, 40:42], small[:, 42:44]
        s_prod, s_root, alpha, neg_shift = (small[:, k:k + 1] for k in (44, 45, 46, 47))

        bank = [ctx.enter_context(nc.psum_tensor(f"bank{i}", [P, BLK], F32)) for i in range(6, 8)]
        score = [ctx.enter_context(nc.psum_tensor(f"score{i}", [P, 2, BLK], F32)) for i in range(SB)]
        bank = [sc[:, e, :] for sc in score for e in range(2)] + [b[:, :] for b in bank]

        AHEAD = 2

        consts_ready, waits_passed = sem("consts_ready"), sem("waits_passed")
        zeroed = sem("zeroed")
        x_in = [sem(f"x_in{g}") for g in range(AHEAD + 1)]
        w0_in, adst_in = sem("w0_in"), sem("adst_in")
        stats_done, aggr_done = sem("stats_done"), sem("aggr_done")
        std_done, rstd_done, nmr_done = sem("std_done"), sem("rstd_done"), sem("nmr_done")
        a_h, a_tr, a_ht, a_mm, a_mx = sem("a_h"), sem("a_tr"), sem("a_ht"), sem("a_mm"), sem("a_mx")
        mva_done = sem("mva_done")
        a_prod, a_t = sem("a_prod"), sem("a_t")
        a_mabs, b_seq, b_flag = sem("a_mabs"), sem("b_seq"), sem("b_flag")
        ext_done, ext_all_done = sem("ext_done"), sem("ext_all_done")
        tsub_done, exp_done = sem("tsub_done"), sem("exp_done")
        e_zero = sem("e_zero")
        e_hi, e_rest, e_mid, e_low = (sem(n) for n in ("e_hi", "e_rest", "e_mid", "e_low"))
        b_val, b_hi, b_rest, b_mid, b_low = (sem(n) for n in ("b_val", "b_hi", "b_rest", "b_mid", "b_low"))
        adj_in = [sem(f"adj_in{c}") for c in range(CH)]
        c_cast, c_tr, c_adjt, c_mm, c_acc = (sem(n) for n in ("c_cast", "c_tr", "c_adjt", "c_mm", "c_acc"))
        xt_in = [sem(f"xt_in{u}") for u in range(2)]
        adjt_out = [sem(f"adjt_out{u}") for u in range(2)]
        c_den, c_rden, c_att, c_x1, c_stat, c_aggr = (sem(n) for n in ("c_den", "c_rden", "c_att", "c_x1", "c_stat", "c_aggr"))
        x1_out, c_mv = sem("x1_out"), sem("c_mv")
        wq_in, wk_in, wv_in, wo_in = (sem(n) for n in ("wq_in", "wk_in", "wv_in", "wo_in"))
        d_wsq, d_wnorm, d_wmax, d_wrt, d_wsc, d_scales = (sem(n) for n in ("d_wsq", "d_wnorm", "d_wmax", "d_wrt", "d_wsc", "d_scales"))
        d_h, d_tr, d_ht, d_v, d_vout = (sem(n) for n in ("d_h", "d_tr", "d_ht", "d_v", "d_vout"))
        d_qk, d_hi, d_lo, d_sq, d_nrm, d_nmax = (sem(n) for n in ("d_qk", "d_hi", "d_lo", "d_sq", "d_nrm", "d_nmax"))
        hi_out = [sem(f"hi_out{b}") for b in range(4)]
        lo_out = [sem(f"lo_out{b}") for b in range(4)]
        d_nm2, d_nm2_all, d_sprod, d_root, d_shift = (sem(n) for n in ("d_nm2", "d_nm2_all", "d_sprod", "d_root", "d_shift"))
        q_in = [sem(f"q_in{r}") for r in range(PAIRS)]
        mask_in = [sem(f"mask_in{c}") for c in range(CH)]
        s_ready, s_exp, p_masked, pv_done, sum_done, den_done = (sem(n) for n in ("s_ready", "s_exp", "p_masked", "pv_done", "sum_done", "den_done"))
        pair_added = sem("pair_added")
        o_copied, rden_done, ot_done, wo_done, out_ready = (sem(n) for n in ("o_copied", "rden_done", "ot_done", "wo_done", "out_ready"))
        xo_in = [sem(f"xo_in{b}") for b in range(2)]
        out_stored = [sem(f"out_stored{b}") for b in range(2)]

        STEPS = PAIRS * NT
        GROUPS = STEPS // SG
        SUMS = SG - 2

        after = {13: 0, 18: 1, 23: 2, 28: 3}
        ring = []
        for k in range(STEPS):
            ring.append(("scores", k))
            if k in after:
                ring.append(("output", after[k]))
        assert len(ring) % SB == 0 and len(after) == TB

        def settled(engine):
            engine.sem_inc(waits_passed, 1)

        block = ctx.enter_context(nc.Block())

        @block.sync
        def _(sp):
            for b in range(4):
                sp.sem_inc(hi_out[b], 32)
                sp.sem_inc(lo_out[b], 32)
            for g in range(NB):
                sp.dma_start(nodes[:, g * TB:(g + 1) * TB, :],
                             x[g * BLK:(g + 1) * BLK, :].rearrange("(t p) d -> p t d", p=P)).then_inc(x_in[min(g, AHEAD)], 16)
                if g == 0:
                    for c in range(FC):
                        sp.dma_start(w0_sb[:, c, :].rearrange("p (h d) -> p h d", h=H),
                                     w0[:, c * P:(c + 1) * P, :].rearrange("h p d -> p h d")).then_inc(w0_in, 16)
                    sp.dma_start(adst, a_dst.rearrange("(o h) d -> o (h d)", o=1).broadcast_to([P, D])).then_inc(adst_in, 16)

            def load_adj(n, c):
                sp.wait_ge(c_cast, CH * n + c + 1)
                settled(sp)
                sp.dma_start(adjf[:, c, :], adj[bass.ds(n * P, P), c * CW:(c + 1) * CW]).then_inc(adj_in[c], 16)

            def load_x(t, u):
                sp.wait_ge(c_x1, t + 1)
                settled(sp)
                sp.dma_start(xt[:, u, :], x[bass.ds(t * P, P), :]).then_inc(xt_in[u], 16)

            for u in range(2):
                sp.sem_inc(adjt_out[u], 16)

            def store_adjt(n, u):
                sp.wait_ge(c_adjt, CH + CH * (n + 1))
                settled(sp)
                sp.dma_start(adjt_dram[bass.ds(n, 1), :, :].rearrange("o p n -> (o p) n"), adjt_bytes[:, u, :]).then_inc(adjt_out[u], 16)

            def store_x1(t):
                sp.wait_ge(c_x1, 2 + t + 1)
                settled(sp)
                sp.dma_start(x1_dram[bass.ds(t * P, P), :],
                             nodes[:, bass.ds(t, 1), :].rearrange("p o d -> p (o d)")).then_inc(x1_out, 16)

            for c in range(CH):
                load_adj(0, c)
            for c in range(CH):
                load_adj(1, c)
            load_x(0, 0)
            store_adjt(0, 0)
            with sp.Fori(0, NT // 2 - 1) as i:
                for u in range(2):
                    t = 2 * i + u
                    load_x(t + 1, 1 - u)
                    for c in range(CH):
                        load_adj(t + 2, c)
                    store_adjt(t + 1, 1 - u)
                    store_x1(t)
            load_x(NT - 1, 1)
            store_adjt(NT - 1, 1)
            store_x1(NT - 2)
            store_x1(NT - 1)

            def load_w(dst, w, s, by_head):
                for c in range(FC):
                    src = w[:, c * P:(c + 1) * P, :].rearrange("h p d -> p h d") if by_head else \
                        w[2 * c:2 * c + 2, :, :].rearrange("h d n -> (h d) n")
                    to = dst[:, c, :].rearrange("p (h d) -> p h d", h=H) if by_head else dst[:, c, :]
                    sp.dma_start(to, src).then_inc(s, 16)

            sp.wait_ge(c_cast, CH + CH * NT)
            load_w(wq_sb, wq, wq_in, True)
            load_w(wk_sb, wk, wk_in, True)
            sp.wait_ge(c_tr, CH + CH * NT)
            load_w(wv_sb, wv, wv_in, True)
            sp.wait_ge(c_mm, 2 + NT)
            for u in range(2):
                sp.wait_ge(adjt_out[u], 16 * (NT // 2 + 1))
            load_w(wo_sb, wo, wo_in, False)

            def store_qk(g, idx):
                b, pair = idx % 4, idx % PAIRS
                for what, done, credit, stored, half in ((hi, d_hi, 0, hi_out, 0), (lo, d_lo, 2, lo_out, 1)):
                    sp.wait_ge(done, credit + g * 8 + idx + 1)
                    settled(sp)
                    for e in range(2):
                        src = what[e * HD:(e + 1) * HD, b, :]
                        if idx < PAIRS:
                            dst = keys[half * HD:(half + 1) * HD, 2 * pair + e, bass.ds(g * BLK, BLK)]
                        else:
                            dst = q_dram[bass.ds(g, 1), half, 2 * pair + e, :, :].rearrange("o d n -> (o d) n")
                        sp.dma_start(dst, src).then_inc(stored[b], 16)

            with sp.Fori(0, NB) as g:
                for idx in range(8):
                    store_qk(g, idx)
            for b in range(4):
                sp.wait_ge(hi_out[b], 32 * (2 * NB + 1))
                sp.wait_ge(lo_out[b], 32 * (2 * NB + 1))

            sp.wait_ge(d_v, 2 + NT)
            sp.wait_ge(d_nm2, 2)

            def load_q(qb, r):
                sp.wait_ge(s_ready, STEPS * qb + NT * (r + 1))
                settled(sp)
                for half in range(2):
                    for s in range(2):
                        sp.dma_start(qs[half * HD:(half + 1) * HD, r, s, :, :],
                                     q_dram[bass.ds(qb, 1), s, 2 * r:2 * r + 2, :, :].rearrange("o h d n -> (o d) h n")
                                     ).then_inc(q_in[r], 16)

            def load_mask(qb, c):
                sp.wait_ge(p_masked, STEPS * qb + STEPS - NT + KC * (c + 1))
                settled(sp)
                sp.dma_start(mask[:, :, c * KC:(c + 1) * KC, :].rearrange("p t k n -> p t (k n)"),
                             adjt_dram[bass.ds(qb * TB, TB), :, c * CW:(c + 1) * CW].rearrange("t p n -> p t n")
                             ).then_inc(mask_in[c], 16)

            def load_block(qb):
                load_q(qb, 0)
                load_q(qb, 1)
                load_q(qb, 2)
                for c in range(CH - 1):
                    load_mask(qb, c)
                load_q(qb, 3)
                load_mask(qb, CH - 1)

            def load_x1(qb, r):
                sp.wait_ge(out_stored[r % 2], 16 * (2 * qb + r // 2 + 1))
                settled(sp)
                sp.dma_start(xo[:, r % 2, :], x1_dram[bass.ds(qb * BLK + r * P, P), :]).then_inc(xo_in[r % 2], 16)

            def store_out(qb, r):
                sp.wait_ge(out_ready, TB * qb + r + 1)
                settled(sp)
                sp.dma_start(out[bass.ds(qb * BLK + r * P, P), :], xo[:, r % 2, :]).then_inc(out_stored[r % 2], 16)

            def finish_block(qb):
                load_x1(qb, 0)
                load_x1(qb, 1)
                store_out(qb, 0)
                load_x1(qb, 2)
                store_out(qb, 1)
                load_x1(qb, 3)
                store_out(qb, 2)
                store_out(qb, 3)

            for b in range(2):
                sp.sem_inc(out_stored[b], 16)
            load_block(0)
            with sp.Fori(1, NB) as qb:
                load_block(qb)
                finish_block(qb - 1)
            finish_block(NB - 1)
            for b in range(2):
                sp.wait_ge(out_stored[b], 16 * (2 * NB + 1))

        @block.gpsimd
        def _(pool):
            nc.gpsimd.memset(identf[:, :], 0.0).then_inc(zeroed, 1)
            nc.gpsimd.memset(identb[:, :], 0.0).then_inc(zeroed, 1)
            nc.gpsimd.memset(onesf[:, :], 1.0).then_inc(consts_ready, 1)
            nc.gpsimd.memset(eps_c, EPS).then_inc(consts_ready, 1)
            nc.gpsimd.memset(esplit[:, :, 2, :], 0.0).then_inc(e_zero, 1)
            pool.wait_ge(zeroed, 2)
            for m in (identf, identb):
                nc.gpsimd.affine_select(out=m[:, :], in_=m[:, :], compare_op=ALU.not_equal, fill=1.0, base=0,
                                        pattern=[[-1, P]], channel_multiplier=1).then_inc(consts_ready, 1)

            pool.wait_ge(ext_done, 3)
            nc.gpsimd.partition_all_reduce(ext_all[:, :], ext[:, :], P, RMAX).then_inc(ext_all_done, 1)

            pool.sem_inc(d_sq, 4)
            with pool.Fori(0, NB) as g:
                for idx in range(8):
                    pool.wait_ge(d_hi, g * 8 + idx + 1)
                    pool.wait_ge(d_nrm, g * 8 + idx + 1)
                    nc.gpsimd.tensor_tensor(sq[:, idx % 2, :], hi[:, idx % 4, :], hi[:, idx % 4, :], ALU.mult).then_inc(d_sq, 1)
            pool.wait_ge(d_nm2, 2)
            nc.gpsimd.partition_all_reduce(nm2_all, nm2, P, RMAX).then_inc(d_nm2_all, 1)

            pool.sem_inc(sum_done, SUMS)
            with pool.Fori(0, NB) as qb:
                for k in range(STEPS):
                    b, g = k % SG, k // SG
                    if b < 2:
                        continue
                    pool.wait_ge(p_masked, STEPS * (qb + 1) + k + 1)
                    if b == 2:
                        pool.wait_ge(pair_added, GROUPS * qb + g + 1)
                    else:
                        pool.wait_ge(sum_done, SUMS * (GROUPS * qb + g + 1) + b - 2)
                    nc.gpsimd.tensor_tensor(psums[:, g % 2, :, :], psums[:, g % 2, :, :], prob[:, k % PB, :, :],
                                            ALU.add).then_inc(sum_done, 1)

        @block.scalar
        def _(act):
            act.wait_ge(consts_ready, 8)
            act.sem_inc(a_mx, 2)

            def std_a(g):
                act.wait_ge(aggr_done, TB * (g + 1))
                settled(act)
                nc.scalar.activation(std[:, bass.ds(g * TB, TB)], mv[:, bass.ds(g * TB, TB), 1], ACT.Sqrt, bias=eps_c).then_inc(std_done, 1)

            def norm_a(g, j):
                t = g * TB + j
                if j == 0:
                    act.wait_ge(nmr_done, g + 1)
                act.wait_ge(a_tr, t + 1)
                nc.scalar.activation(ha[:, j, :], nodes[:, bass.ds(t, 1), :].rearrange("p o d -> p (o d)"), ACT.Relu,
                                     bias=nmr[:, bass.ds(t, 1)], scale=rstd[:, bass.ds(t, 1)]).then_inc(a_h, 1)

            def block_a(g, more_stats, more):
                if more_stats:
                    std_a(g + AHEAD)
                for j in range(TB):
                    t = g * TB + j
                    if more:
                        norm_a(g + 1, j)
                    act.wait_ge(a_mm, 2 + t + 1)
                    settled(act)
                    nc.scalar.copy(nodes[:, bass.ds(t, 1), :].rearrange("p o d -> p (o d)"), bank[2 + j % 2]).then_inc(a_mx, 1)

            for g in range(AHEAD):
                std_a(g)
                if g == 0:
                    for j in range(TB):
                        norm_a(0, j)
            with act.Fori(0, NB - AHEAD) as g:
                block_a(g, True, True)
            block_a(NB - 2, False, True)
            block_a(NB - 1, False, False)

            act.sem_inc(c_adjt, CH)

            def adjt_piece(n, u, c):
                act.wait_ge(c_tr, CH + CH * n + c + 1)
                settled(act)
                nc.scalar.activation(adjt[:, u, c * CW:(c + 1) * CW], bank[4 + c].bitcast(BF16), ACT.Copy,
                                     saturate=False).then_inc(c_adjt, 1)

            def adjt_tile(n, u, i):
                act.wait_ge(c_mm, n + 1)
                act.wait_ge(adjt_out[u], 16 * (i + 1))
                for c in range(CH):
                    adjt_piece(n, u, c)

            adjt_tile(0, 0, 0)

            act.wait_ge(tsub_done, 1)
            nc.scalar.activation(expt, tall, ACT.Exp, bias=room_c).then_inc(exp_done, 1)
            act.wait_ge(exp_done, 1)
            act.wait_ge(b_flag, 1)
            is_wide = act.value_load(wide_range[0:1, 0:1], min_val=0, max_val=1)
            with act.If(is_wide > 0):
                nc.scalar.activation(esplit[:, :, 0, :], expt, ACT.Copy, scale=E_TOP).then_inc(e_hi, 1)
                act.wait_ge(e_rest, 1)
                nc.scalar.copy(esplit[:, :, 1, :], erest).then_inc(e_mid, 1)
                for g in range(NB + 1):
                    if g < NB:
                        act.wait_ge(b_val, g + 1)
                        nc.scalar.copy(emx[:, g * TB:(g + 1) * TB, 0, :], nodes[:, g * TB:(g + 1) * TB, :]).then_inc(b_hi, 1)
                    if g >= 1:
                        act.wait_ge(b_rest, g)
                        nc.scalar.copy(emx[:, (g - 1) * TB:g * TB, 1, :], nodes[:, (g - 1) * TB:g * TB, :]).then_inc(b_mid, 1)
            with act.Else():
                nc.scalar.activation(esplit_pair[:, :, 0, :], expt, ACT.Copy, scale=E_TOP).then_inc(e_hi, 1)
                for g in range(NB):
                    act.wait_ge(b_val, g + 1)
                    nc.scalar.copy(emx_pair[:, g * TB:(g + 1) * TB, 0, :], nodes[:, g * TB:(g + 1) * TB, :]).then_inc(b_hi, 1)

            with act.Fori(0, NT // 2 - 1) as i:
                adjt_tile(2 * i + 1, 1, i)
                adjt_tile(2 * i + 2, 0, i + 1)
            adjt_tile(NT - 1, 1, NT // 2 - 1)

            act.wait_ge(c_mv, NT)
            nc.scalar.activation(std[:, :], mv[:, :, 1], ACT.Sqrt, bias=eps_c).then_inc(std_done, 1)
            act.sem_inc(d_vout, 2)

            def norm_tile(t, j):
                act.wait_ge(d_tr, t + 1)
                nc.scalar.activation(hd[:, j % 2, :], nodes[:, bass.ds(t, 1), :].rearrange("p o d -> p (o d)"), ACT.Relu,
                                     bias=nmr[:, bass.ds(t, 1)], scale=rstd[:, bass.ds(t, 1)]).then_inc(d_h, 1)

            act.wait_ge(nmr_done, NB + 1)
            act.wait_ge(x1_out, 16 * NT)
            for j in range(TB):
                norm_tile(j, j)
            act.wait_ge(d_wmax, 2)
            nc.scalar.activation(wrt, wmax, ACT.Sqrt, scale=float(D)).then_inc(d_wrt, 1)
            act.wait_ge(d_scales, 1)

            def project(g, last):
                for j in range(TB):
                    t = g * TB + j
                    if not last:
                        norm_tile(t + TB, j)
                    act.wait_ge(d_v, 2 + t + 1)
                    settled(act)
                    nc.scalar.copy(nodes[:, bass.ds(t, 1), :].rearrange("p o d -> p (o d)"), bank[2 + j % 2]).then_inc(d_vout, 1)
                for idx in range(8):
                    act.wait_ge(d_qk, 2 + g * 8 + idx + 1)
                    act.wait_ge(hi_out[idx % 4], 32 * (2 * g + idx // 4 + 1))
                    act.wait_ge(d_sq, g * 8 + idx + 1)
                    kind = 1 if idx < PAIRS else 0
                    nc.scalar.activation(hi[:, idx % 4, :], bank[4 + idx % 2], ACT.Copy,
                                         scale=wsc[:, kind:kind + 1]).then_inc(d_hi, 1)

            with act.Fori(0, NB - 1) as g:
                project(g, False)
            project(NB - 1, True)
            act.wait_ge(d_sprod, 1)
            nc.scalar.activation(s_root, s_prod, ACT.Sqrt).then_inc(d_root, 1)

            act.wait_ge(d_shift, 1)
            act.sem_inc(o_copied, 1)

            def copy_attention(qb, r):
                if r == 0:
                    act.wait_ge(wo_done, TB * qb)
                act.wait_ge(pv_done, PB + STEPS * qb + (r + 1) * NT)
                nc.scalar.copy(ot[:, r, :], bank[6]).then_inc(o_copied, 1)

            def exps(qb, first):
                for at, (kind, k) in enumerate(ring):
                    if kind == "output":
                        continue
                    act.wait_ge(s_ready, STEPS * (qb + 1) + k + 1)
                    sc = score[at % SB][:, :, :]
                    nc.scalar.activation(sc, sc, ACT.Exp, bias=neg_shift, scale=alpha).then_inc(s_exp, 1)
                    if k % NT == 1 and k > NT:
                        if k // NT == 1 and first:
                            act.wait_ge(pv_done, PB + NT)
                            nc.scalar.copy(ot[:, 0, :], bank[6]).then_inc(o_copied, 1)
                        else:
                            copy_attention(qb, k // NT - 1)
                    elif k == 1 and not first:
                        copy_attention(qb - 1, PAIRS - 1)

            exps(0, True)
            with act.Fori(1, NB) as qb:
                exps(qb, False)
            copy_attention(NB - 1, PAIRS - 1)

        @block.vector
        def _(dve):
            for e in range(2):
                for f in range(2):
                    nc.vector.memset(headones[e * HD:(e + 1) * HD, f * HD:(f + 1) * HD], float(e == f)).then_inc(consts_ready, 1)
            dve.sem_inc(a_ht, 2)
            dve.sem_inc(c_cast, CH)
            dve.sem_inc(c_acc, 2)
            dve.sem_inc(c_x1, 2)

            def stats_a(g):
                for j in range(TB):
                    t = g * TB + j
                    nc.vector.bn_stats(stats[:, j, :], nodes[:, bass.ds(t, 1), :].rearrange("p o d -> p (o d)")).then_inc(stats_done, 1)
                for j in range(TB):
                    t = g * TB + j
                    dve.wait_ge(stats_done, t + 1)
                    settled(dve)
                    nc.vector.bn_aggr(mva[:, j, :], stats[:, j, :]).then_inc(mva_done, 1)
                dve.wait_ge(mva_done, TB * (g + 1))
                nc.vector.tensor_copy(mv[:, bass.ds(g * TB, TB), :], mva[:, :, :]).then_inc(aggr_done, TB)

            def factors_a(g):
                cols = bass.ds(g * TB, TB)
                dve.wait_ge(std_done, g + 1)
                settled(dve)
                nc.vector.reciprocal(rstd[:, cols], std[:, cols]).then_inc(rstd_done, 1)
                dve.wait_ge(rstd_done, g + 1)
                settled(dve)
                nc.vector.scalar_tensor_tensor(out=nmr[:, cols], in0=mv[:, cols, 0], scalar=-1.0, in1=rstd[:, cols],
                                               op0=ALU.mult, op1=ALU.mult).then_inc(nmr_done, 1)

            def copy_ha(t, j):
                dve.wait_ge(a_tr, TB + t + 1)
                dve.wait_ge(a_mm, t + 1)
                nc.vector.tensor_copy(hta[:, j % 2, :, :], bank[j % 2].rearrange("p (c n) -> p c n", c=FC)).then_inc(a_ht, 1)

            def logits_a(t, j):
                dve.wait_ge(a_mx, 2 + t + 1)
                nc.vector.tensor_tensor(prod[:, j % 2, :], nodes[:, bass.ds(t, 1), :].rearrange("p o d -> p (o d)"),
                                        adst, ALU.mult).then_inc(a_prod, 1)
                nc.vector.tensor_reduce(mabs[:, bass.ds(t, 1)], nodes[:, bass.ds(t, 1), :].rearrange("p o d -> p (o d)"),
                                        AX.X, ALU.max, apply_absolute_value=True).then_inc(a_mabs, 1)
                dve.wait_ge(a_prod, t + 1)
                nc.vector.tensor_reduce(tall[:, bass.ds(t, 1), :].rearrange("p o h -> p (o h)"),
                                        prod[:, j % 2, :].rearrange("p (h d) -> p h d", h=H), AX.X, ALU.add).then_inc(a_t, 1)

            def block_a(g, more_stats, more):
                if more_stats:
                    stats_a(g + AHEAD)
                for j in range(TB):
                    t = g * TB + j
                    if more or j < 2:
                        copy_ha(t + 2, j)
                    logits_a(t, j)
                    if j == 0 and more_stats:
                        factors_a(g + AHEAD)

            def cast_tile(n):
                for c in range(CH):
                    dve.wait_ge(adj_in[c], 16 * (n + 1))
                    dve.wait_ge(c_tr, CH * n + c + 1)
                    nc.vector.tensor_scalar(adjb[:, c, :], adjf[:, c, :], 0.0, EDGE, ALU.is_gt, ALU.mult).then_inc(c_cast, 1)

            for g in range(AHEAD):
                dve.wait_ge(x_in[g], 16)
                stats_a(g)
                factors_a(g)
                if g == 0:
                    copy_ha(0, 0)
                    copy_ha(1, 1)
            dve.wait_ge(adst_in, 16)
            dve.wait_ge(x_in[AHEAD], 16 * (NB - AHEAD))
            with dve.Fori(0, NB - AHEAD) as g:
                block_a(g, True, True)
            cast_tile(0)
            block_a(NB - 2, False, True)
            block_a(NB - 1, False, False)

            def norm_factors(n):
                dve.wait_ge(std_done, n)
                nc.vector.reciprocal(rstd[:, :], std[:, :]).then_inc(rstd_done, 1)
                dve.wait_ge(rstd_done, n)
                nc.vector.scalar_tensor_tensor(out=nmr[:, :], in0=mv[:, :, 0], scalar=-1.0, in1=rstd[:, :],
                                               op0=ALU.mult, op1=ALU.mult).then_inc(nmr_done, 1)

            dve.wait_ge(a_t, NT)
            dve.wait_ge(a_mabs, NT)
            t_by_head = tall.rearrange("p t h -> p h t")
            nc.vector.tensor_reduce(ext[:, 0:H], t_by_head, AX.X, ALU.max).then_inc(ext_done, 1)
            nc.vector.tensor_reduce(ext[:, H:2 * H], t_by_head, AX.X, ALU.min, negate=True).then_inc(ext_done, 1)
            nc.vector.tensor_reduce(ext[:, 2 * H:2 * H + 1], mabs[:, :], AX.X, ALU.max).then_inc(ext_done, 1)
            dve.wait_ge(ext_all_done, 1)
            nc.vector.tensor_tensor(tall, tall, ext_all[:, 0:H].rearrange("p (o h) -> p o h", o=1).broadcast_to([P, NT, H]),
                                    ALU.subtract).then_inc(b_seq, 1)
            nc.vector.tensor_tensor(range8, ext_all[:, 0:H], ext_all[:, H:2 * H], ALU.add).then_inc(b_seq, 1)
            dve.wait_ge(b_seq, 2)
            nc.vector.tensor_reduce(t_range, range8, AX.X, ALU.max).then_inc(b_seq, 1)
            dve.wait_ge(b_seq, 3)
            nc.vector.tensor_scalar(room_c, t_range, NARROW, HEADROOM0, ALU.is_gt, ALU.mult).then_inc(tsub_done, 1)
            nc.vector.tensor_scalar(wide_range[:, :], t_range, NARROW, None, ALU.is_gt).then_inc(b_flag, 1)
            nc.vector.tensor_scalar(mx_over, ext_all[:, 2 * H:2 * H + 1], 1e-24, 1.0 / MX_TOP, ALU.max, ALU.mult).then_inc(b_seq, 1)
            dve.wait_ge(b_seq, 4)
            nc.vector.reciprocal(mx_scale, mx_over).then_inc(b_seq, 1)
            dve.wait_ge(b_seq, 5)
            nc.vector.tensor_scalar(mx_over, mx_over, E_TOP, None, ALU.mult).then_inc(b_seq, 1)
            cast_tile(1)
            dve.wait_ge(exp_done, 1)

            def weigh(g):
                v = nodes[:, g * TB:(g + 1) * TB, :].rearrange("p t (h d) -> p (t h) d", h=H)
                e = expt[:, g * TB:(g + 1) * TB, :].rearrange("p t (h o) -> p (t h) o", o=1).broadcast_to([P, TB * H, HD])
                nc.vector.scalar_tensor_tensor(out=v, in0=v, scalar=mx_scale, in1=e, op0=ALU.mult, op1=ALU.mult).then_inc(b_val, 1)

            def rest(g, high, out, done):
                nc.vector.tensor_tensor(out, nodes[:, g * TB:(g + 1) * TB, :], high[:, g * TB:(g + 1) * TB, 0, :],
                                        ALU.subtract).then_inc(done, 1)

            dve.wait_ge(b_seq, 6)
            dve.wait_ge(b_flag, 1)
            is_wide = dve.value_load(wide_range[0:1, 0:1], min_val=0, max_val=1)
            with dve.If(is_wide > 0):
                dve.wait_ge(e_hi, 1)
                nc.vector.scalar_tensor_tensor(out=erest, in0=expt, scalar=E_TOP, in1=esplit[:, :, 0, :],
                                               op0=ALU.mult, op1=ALU.subtract).then_inc(e_rest, 1)
                for g in range(NB + 1):
                    if g == 1:
                        dve.wait_ge(e_mid, 1)
                        dve.wait_ge(e_zero, 1)
                        nc.vector.tensor_tensor(esplit[:, :, 2, :], erest, esplit[:, :, 1, :], ALU.subtract).then_inc(e_low, 1)
                    if g < NB:
                        weigh(g)
                        dve.wait_ge(b_hi, g + 1)
                        rest(g, emx, nodes[:, g * TB:(g + 1) * TB, :], b_rest)
                    if g >= 1:
                        dve.wait_ge(b_mid, g)
                        nc.vector.tensor_tensor(emx[:, (g - 1) * TB:g * TB, 2, :], nodes[:, (g - 1) * TB:g * TB, :],
                                                emx[:, (g - 1) * TB:g * TB, 1, :], ALU.subtract).then_inc(b_low, 1)
            with dve.Else():
                weigh(0)
                dve.wait_ge(e_hi, 1)
                nc.vector.scalar_tensor_tensor(out=esplit_pair[:, :, 1, :], in0=expt, scalar=E_TOP, in1=esplit_pair[:, :, 0, :],
                                               op0=ALU.mult, op1=ALU.subtract).then_inc(e_low, 1)
                for g in range(NB):
                    if g + 1 < NB:
                        weigh(g + 1)
                    dve.wait_ge(b_hi, g + 1)
                    rest(g, emx_pair, emx_pair[:, g * TB:(g + 1) * TB, 1, :], b_low)

            def finish_tile(t, u, i):
                dve.wait_ge(c_mm, 2 + t + 1)
                nc.vector.tensor_reduce(den8, bank[2 + u][:, 0:3 * H].rearrange("p (s h) -> p h s", s=3), AX.X, ALU.add).then_inc(c_den, 1)
                dve.wait_ge(c_den, t + 1)
                nc.vector.reciprocal(rden8, den8).then_inc(c_rden, 1)
                dve.wait_ge(c_rden, 2 * t + 1)
                nc.vector.tensor_scalar(rden8, rden8, mx_over, None, ALU.mult).then_inc(c_rden, 1)
                dve.wait_ge(c_rden, 2 * t + 2)
                nc.vector.tensor_tensor(att0.rearrange("p (h d) -> p h d", h=H), bank[u].rearrange("p (h d) -> p h d", h=H),
                                        rden8.rearrange("p (h o) -> p h o", o=1).broadcast_to([P, H, HD]),
                                        ALU.mult).then_inc(c_acc, 1)
                dve.wait_ge(c_acc, 2 + t + 1)
                dve.wait_ge(xt_in[u], 16 * (i + 1))
                row = nodes[:, bass.ds(t, 1), :].rearrange("p o d -> p (o d)")
                nc.vector.tensor_tensor(row, att0, xt[:, u, :], ALU.add).then_inc(c_x1, 1)
                dve.wait_ge(c_x1, 2 + t + 1)
                settled(dve)
                nc.vector.bn_stats(stats[:, u, :], row).then_inc(c_stat, 1)
                dve.wait_ge(c_stat, t + 1)
                settled(dve)
                nc.vector.bn_aggr(mv1[:, u, :], stats[:, u, :]).then_inc(c_aggr, 1)
                dve.wait_ge(c_aggr, t + 1)
                nc.vector.tensor_copy(mv[:, bass.ds(t, 1), :].rearrange("p o d -> p (o d)"), mv1[:, u, :]).then_inc(c_mv, 1)

            with dve.Fori(0, NT // 2 - 1) as i:
                for u in range(2):
                    finish_tile(2 * i + u, u, i)
                    cast_tile(2 * i + u + 2)
            for u in range(2):
                finish_tile(NT - 2 + u, u, NT // 2 - 1)

            dve.sem_inc(d_ht, 2)
            dve.sem_inc(d_lo, 2)
            dve.sem_inc(d_nmax, 2)

            def copy_ht(g, j, u):
                t = g * TB + j
                dve.wait_ge(d_tr, 2 + t + 1)
                nc.vector.tensor_copy(htd[:, u, :, j * P:(j + 1) * P], bank[j % 2].rearrange("p (c n) -> p c n", c=FC)).then_inc(d_ht, 1)

            norm_factors(NB + 1)
            for j in range(TB):
                copy_ht(0, j, 0)

            for n, (w, s) in enumerate(((wq_sb, wq_in), (wk_sb, wk_in))):
                dve.wait_ge(s, 16 * FC)
                if n == 1:
                    dve.wait_ge(d_wnorm, 1)
                nc.vector.tensor_tensor(wsq, w.rearrange("p c n -> p (c n)"), w.rearrange("p c n -> p (c n)"), ALU.mult).then_inc(d_wsq, 1)
                dve.wait_ge(d_wnorm, n + 1)
                nc.vector.tensor_reduce(wmax[:, n:n + 1], bank[6 + n], AX.X, ALU.max).then_inc(d_wsc, 1)
            dve.wait_ge(d_wsc, 2)
            nc.vector.tensor_scalar(wmax, wmax, 1e-24, None, ALU.max).then_inc(d_wmax, 2)
            dve.wait_ge(d_wrt, 1)
            nc.vector.reciprocal(wsc, wrt).then_inc(d_wsc, 1)
            dve.wait_ge(d_wsc, 3)
            nc.vector.tensor_scalar(wsc, wsc, QK_TOP, None, ALU.mult).then_inc(d_scales, 1)

            def norms(g, idx):
                kind = 1 if idx < PAIRS else 0
                dve.wait_ge(d_nrm, 2 + g * 8 + idx + 1)
                nc.vector.tensor_reduce(norm_max[:, bass.ds(g * 8 + kind * PAIRS + idx % PAIRS, 1)],
                                        bank[6 + idx % 2], AX.X, ALU.max).then_inc(d_nmax, 1)

            def project(g, u, last):
                if not last:
                    for j in range(TB):
                        copy_ht(g + 1, j, 1 - u)
                for idx in range(8):
                    kind = 1 if idx < PAIRS else 0
                    dve.wait_ge(d_hi, g * 8 + idx + 1)
                    dve.wait_ge(lo_out[idx % 4], 32 * (2 * g + idx // 4 + 1))
                    nc.vector.scalar_tensor_tensor(out=lo[:, idx % 4, :], in0=bank[4 + idx % 2], scalar=wsc[:, kind:kind + 1],
                                                   in1=hi[:, idx % 4, :], op0=ALU.mult, op1=ALU.subtract).then_inc(d_lo, 1)
                    if idx >= 2:
                        norms(g, idx - 2)
                norms(g, 6)
                norms(g, 7)

            with dve.Fori(0, NB // 2 - 1) as i:
                project(2 * i, 0, False)
                project(2 * i + 1, 1, False)
            project(NB - 2, 0, False)
            project(NB - 1, 1, True)

            dve.wait_ge(d_nmax, 2 + 8 * NB)
            for kind in range(2):
                nc.vector.tensor_reduce(nm2[:, kind:kind + 1],
                                        norm_max.rearrange("p (g k r) -> p k g r", g=NB, k=2)[:, kind, :, :],
                                        AX.XY, ALU.max).then_inc(d_nm2, 1)
            dve.wait_ge(d_nm2_all, 1)
            nc.vector.tensor_tensor(s_prod, nm2_all[:, 0:1], nm2_all[:, 1:2], ALU.mult).then_inc(d_sprod, 1)
            nc.vector.tensor_tensor(alpha, wrt[:, 0:1], wrt[:, 1:2], ALU.mult).then_inc(d_wsc, 1)
            dve.wait_ge(d_wsc, 4)
            nc.vector.tensor_scalar(alpha, alpha, 1.0 / (HD ** 0.5 * QK_TOP * QK_TOP), None, ALU.mult).then_inc(d_wsc, 1)
            dve.wait_ge(d_wsc, 5)
            dve.wait_ge(d_root, 1)
            nc.vector.scalar_tensor_tensor(out=neg_shift, in0=s_root, scalar=-1.0, in1=alpha, op0=ALU.mult, op1=ALU.mult).then_inc(d_wsc, 1)
            dve.wait_ge(d_wsc, 6)
            nc.vector.tensor_scalar(neg_shift, neg_shift, HEADROOM1, 0.0, ALU.add, ALU.min).then_inc(d_shift, 1)

            dve.sem_inc(p_masked, STEPS)
            dve.sem_inc(ot_done, 1)

            def invert(qb, r, j):
                if j == 0:
                    dve.wait_ge(den_done, 2 + GROUPS * qb + (r + 1) * NT // SG)
                part_of = bank[7][:, j * P:(j + 1) * P]
                nc.vector.reciprocal(part_of, part_of).then_inc(rden_done, 1)

            def divide(qb, r):
                dve.wait_ge(rden_done, TB * (PAIRS * qb + r + 1))
                dve.wait_ge(o_copied, 1 + PAIRS * qb + r + 1)
                nc.vector.tensor_tensor(ot[:, r, :], ot[:, r, :], bank[7], ALU.mult).then_inc(ot_done, 1)

            def add_x1(qb, r, src):
                dve.wait_ge(wo_done, TB * qb + r + 1)
                dve.wait_ge(xo_in[r % 2], 16 * (2 * qb + r // 2 + 1))
                nc.vector.tensor_tensor(xo[:, r % 2, :], xo[:, r % 2, :], src, ALU.add).then_inc(out_ready, 1)

            def masks(qb, first):
                for at, (kind, k) in enumerate(ring):
                    if kind == "output":
                        if not first:
                            add_x1(qb - 1, k, score[at % SB][:, 0, :])
                        continue
                    r, kt = k // NT, k % NT
                    if r == 0 and kt % KC == 0:
                        dve.wait_ge(mask_in[kt // KC], 16 * (qb + 1))
                    dve.wait_ge(s_exp, STEPS * qb + k + 1)
                    dve.wait_ge(pv_done, STEPS * qb + k + 1)
                    g, b = (k - PB) // SG, (k - PB) % SG
                    if b < 2:
                        dve.wait_ge(pair_added, GROUPS * qb + g + 1)
                    else:
                        dve.wait_ge(sum_done, SUMS * (GROUPS * qb + g + 1) + b - 1)
                    nc.vector.tensor_tensor(prob[:, k % PB, :, :].rearrange("p h (t n) -> p h t n", t=TB),
                                            score[at % SB][:, :, :].rearrange("p h (t n) -> p h t n", t=TB),
                                            mask[:, :, kt, :].unsqueeze(1).broadcast_to([P, 2, TB, P]), ALU.mult).then_inc(p_masked, 1)
                    if k % SG == 1:
                        g = k // SG
                        dve.wait_ge(p_masked, STEPS * (qb + 1) + k + 1)
                        dve.wait_ge(den_done, GROUPS * qb + g + 1)
                        nc.vector.tensor_tensor(psums[:, g % 2, :, :], prob[:, (k - 1) % PB, :, :], prob[:, k % PB, :, :],
                                                ALU.add).then_inc(pair_added, 1)
                    if (r or not first) and kt in (4, 5, 6, 7, 8):
                        done = (qb, r - 1) if r else (qb - 1, PAIRS - 1)
                        if kt < 8:
                            invert(*done, kt - 4)
                        else:
                            divide(*done)

            masks(0, True)
            with dve.Fori(1, NB) as qb:
                masks(qb, False)
            for j in range(TB):
                invert(NB - 1, PAIRS - 1, j)
            divide(NB - 1, PAIRS - 1)
            for r in range(TB):
                add_x1(NB - 1, r, score[r % SB][:, 0, :])

        @block.tensor
        def _(pe):
            pe.wait_ge(consts_ready, 8)
            pe.sem_inc(a_tr, TB)
            pe.sem_inc(a_mm, 2)
            pe.sem_inc(c_tr, CH)
            pe.sem_inc(c_mm, 2)
            pe.sem_inc(d_tr, 2)
            pe.sem_inc(d_v, 2)
            pe.sem_inc(d_qk, 2)
            pe.sem_inc(d_nrm, 2)

            def transpose_a(t, j):
                pe.wait_ge(a_h, t + 1)
                pe.wait_ge(a_ht, t + 1)
                for c in range(FC):
                    last = nc.tensor.transpose(bank[j % 2][:, c * P:(c + 1) * P], ha[:, j % TB, c * P:(c + 1) * P], identf[:, :])
                last.then_inc(a_tr, 1)

            def block_a(g, more):
                for j in range(TB):
                    t = g * TB + j
                    if more or j < 2:
                        transpose_a(t + 2, j + 2)
                    pe.wait_ge(a_ht, 2 + t + 1)
                    pe.wait_ge(a_mx, t + 1)
                    for c in range(FC):
                        last = nc.tensor.matmul(bank[2 + j % 2], hta[:, j % 2, c, :], w0_sb[:, c, :], start=c == 0, stop=c == FC - 1)
                    last.then_inc(a_mm, 1)

            transpose_a(0, 0)
            transpose_a(1, 1)
            pe.wait_ge(w0_in, 16 * FC)
            with pe.Fori(0, NB - 1) as g:
                block_a(g, True)
            block_a(NB - 1, False)

            def transpose_adj(n, c):
                pe.wait_ge(c_cast, CH + CH * n + c + 1)
                pe.wait_ge(c_adjt, CH * n + c + 1)
                for k in range(KC):
                    last = nc.tensor.transpose(bank[4 + c].bitcast(BF16)[:, k * P:(k + 1) * P], adjb[:, c, k * P:(k + 1) * P], identb[:, :])
                last.then_inc(c_tr, 1)

            for c in range(CH):
                transpose_adj(0, c)
            pe.wait_ge(e_low, 1)
            pe.wait_ge(e_zero, 1)

            def attend(t, u, last_tile, emx_parts, e_parts, parts):
                pe.wait_ge(c_acc, t + 1)
                for c in range(CH):
                    pe.wait_ge(b_low, (c + 1) * NB // CH)
                    pe.wait_ge(c_adjt, CH + CH * t + c + 1)
                    settled(pe)
                    for k in range(c * KC, (c + 1) * KC):
                        first, last_k = k == 0, k == NT - 1
                        w = adjt[:, u, k * P:(k + 1) * P]
                        for s in range(parts):
                            nc.tensor.matmul(bank[u], w, emx_parts[:, k, s, :], start=first and s == 0, stop=last_k and s == parts - 1)
                        last = nc.tensor.matmul(bank[2 + u][:, 0:3 * H], w, e_parts[:, k, :, :].rearrange("p s h -> p (s h)"),
                                                start=first, stop=last_k)
                    if c == CH - 1:
                        last.then_inc(c_mm, 1)
                    if not last_tile:
                        transpose_adj(t + 1, c)

            def attend_all(*how):
                with pe.Fori(0, NT // 2 - 1) as i:
                    for u in range(2):
                        attend(2 * i + u, u, False, *how)
                attend(NT - 2, 0, False, *how)
                attend(NT - 1, 1, True, *how)

            pe.wait_ge(b_flag, 1)
            is_wide = pe.value_load(wide_range[0:1, 0:1], min_val=0, max_val=1)
            with pe.If(is_wide > 0):
                attend_all(emx, esplit, 3)
            with pe.Else():
                attend_all(emx_pair, esplit_pair, 2)

            def transpose_d(g, j):
                t = g * TB + j
                pe.wait_ge(d_h, t + 1)
                pe.wait_ge(d_ht, t + 1)
                for c in range(FC):
                    last = nc.tensor.transpose(bank[j % 2][:, c * P:(c + 1) * P], hd[:, j % 2, c * P:(c + 1) * P], identf[:, :])
                last.then_inc(d_tr, 1)

            def project(g, u, last_block):
                pe.wait_ge(d_ht, 2 + TB * (g + 1))
                for j in range(TB):
                    t = g * TB + j
                    pe.wait_ge(d_vout, t + 1)
                    for c in range(FC):
                        last = nc.tensor.matmul(bank[2 + j % 2], htd[:, u, c, j * P:(j + 1) * P], wv_sb[:, c, :], start=c == 0, stop=c == FC - 1)
                    last.then_inc(d_v, 1)
                    if not last_block:
                        transpose_d(g + 1, j)

                def norm(idx):
                    pe.wait_ge(d_sq, 4 + g * 8 + idx + 1)
                    pe.wait_ge(d_nmax, g * 8 + idx + 1)
                    nc.tensor.matmul(bank[6 + idx % 2], headones[:, :], sq[:, idx % 2, :], start=True, stop=True).then_inc(d_nrm, 1)

                for idx in range(8):
                    w = wk_sb if idx < PAIRS else wq_sb
                    pair = idx % PAIRS
                    pe.wait_ge(d_lo, g * 8 + idx + 1)
                    for c in range(FC):
                        last = nc.tensor.matmul(bank[4 + idx % 2], w[:, c, pair * P:(pair + 1) * P], htd[:, u, c, :], start=c == 0, stop=c == FC - 1)
                    last.then_inc(d_qk, 1)
                    if idx >= 2:
                        norm(idx - 2)
                norm(6)
                norm(7)

            for j in range(TB):
                transpose_d(0, j)
            for n in range(2):
                pe.wait_ge(d_wsq, n + 1)
                for c in range(FC):
                    last = nc.tensor.matmul(bank[6 + n], onesf[:, :], wsq[:, c * D:(c + 1) * D], start=c == 0, stop=c == FC - 1)
                last.then_inc(d_wnorm, 1)
            pe.wait_ge(wv_in, 16 * FC)
            with pe.Fori(0, NB // 2 - 1) as i:
                project(2 * i, 0, False)
                project(2 * i + 1, 1, False)
            project(NB - 2, 0, False)
            project(NB - 1, 1, True)

            pe.sem_inc(s_ready, STEPS)
            pe.sem_inc(pv_done, PB)
            pe.sem_inc(den_done, 2)
            pe.wait_ge(d_vout, 2 + NT)
            pe.wait_ge(d_shift, 1)
            pe.wait_ge(wo_in, 16 * FC)

            def scores(qb, k, buf):
                r, kt = k // NT, k % NT
                if kt == 0:
                    pe.wait_ge(q_in[r], 64 * (qb + 1))
                for e in range(2):
                    for s in range(2):
                        last = nc.tensor.matmul(score[buf][:, e, :], keys[:, 2 * r + e, kt * P:(kt + 1) * P],
                                                qs[:, r, s, e, :], start=s == 0, stop=s == 1)
                last.then_inc(s_ready, 1)

            def output(qb, r, buf):
                pe.wait_ge(ot_done, 1 + PAIRS * (qb + 1))
                for c in range(PAIRS):
                    last = nc.tensor.matmul(score[buf][:, 0, :], ot[:, c, r * P:(r + 1) * P], wo_sb[:, c, :],
                                            start=c == 0, stop=c == PAIRS - 1)
                last.then_inc(wo_done, 1)

            def values(qb, k):
                r, kt = k // NT, k % NT
                if kt == 0:
                    pe.wait_ge(o_copied, PAIRS * qb + r + 1)
                pe.wait_ge(p_masked, STEPS * (qb + 1) + k + 1)
                for e in range(2):
                    last = nc.tensor.matmul(bank[6][e * HD:(e + 1) * HD, :],
                                            nodes[:, kt, (2 * r + e) * HD:(2 * r + e + 1) * HD],
                                            prob[:, k % PB, e, :], start=kt == 0, stop=kt == NT - 1)
                last.then_inc(pv_done, 1)

            def denominators(qb, g):
                r, first, last_group = g // (NT // SG), g % (NT // SG) == 0, (g + 1) % (NT // SG) == 0
                if first:
                    pe.wait_ge(ot_done, PAIRS * qb + r + 1)
                pe.wait_ge(sum_done, SUMS * (GROUPS * qb + g + 2))
                for e in range(2):
                    last = nc.tensor.matmul(bank[7][e * HD:(e + 1) * HD, :], onesf[:, 0:HD], psums[:, g % 2, e, :],
                                            start=first, stop=last_group)
                last.then_inc(den_done, 1)

            def attention(qb, first):
                for at in range(len(ring)):
                    before, k = ring[at - SB]
                    if at < SB:
                        if not first:
                            values(qb - 1, k)
                    elif before == "scores":
                        values(qb, k)
                        if k % SG == 2 and k > SG:
                            denominators(qb, k // SG - 1)
                        elif k == 2 and not first:
                            denominators(qb - 1, GROUPS - 1)
                    elif not first:
                        pe.wait_ge(out_ready, TB * (qb - 1) + k + 1)
                    kind, k = ring[at]
                    if kind == "scores":
                        scores(qb, k, at % SB)
                    elif not first:
                        output(qb - 1, k, at % SB)

            attention(0, True)
            with pe.Fori(1, NB) as qb:
                attention(qb, False)
            for at in range(-SB, 0):
                values(NB - 1, ring[at][1])
            denominators(NB - 1, GROUPS - 1)
            for r in range(TB):
                if r >= SB:
                    pe.wait_ge(out_ready, TB * (NB - 1) + r - SB + 1)
                output(NB - 1, r, r % SB)


_INS = ["x", "adj", "L0_gnn_W", "L0_gnn_a_dst", "L1_gnn_Wks", "L1_gnn_Wqs", "L1_gnn_Wvs", "L1_gnn_Wo"]


def kernel(x, adj, L0_gnn_W, L0_gnn_a_origin, L0_gnn_a_dst, L1_gnn_Wks, L1_gnn_Wqs, L1_gnn_Wvs, L1_gnn_Wo):
    import numpy as _np
    import concourse.bacc as _bacc
    from concourse import mybir as _mybir
    from concourse.bass_utils import run_bass_kernel_spmd as _run

    given = dict(zip(_INS, (x, adj, L0_gnn_W, L0_gnn_a_dst, L1_gnn_Wks, L1_gnn_Wqs, L1_gnn_Wvs, L1_gnn_Wo)))
    nc = _bacc.Bacc("TRN2", target_bir_lowering=False, num_devices=1)
    arrays, args = {}, []
    for name in _INS:
        a = _np.ascontiguousarray(given[name])
        arrays[f"in_{name}_dram"] = a
        args.append(nc.dram_tensor(f"in_{name}_dram", a.shape, _mybir.dt.from_np(a.dtype), kind="ExternalInput").ap())
    out = nc.dram_tensor("out_0_dram", (N, D), F32, kind="ExternalOutput").ap()
    graph_layers(nc, *args, out)
    r = _run(nc, [arrays], core_ids=[0])
    return r.results[0]["out_0_dram"]
```

```python
import concourse.bass as bass
from concourse import mybir
from contextlib import ExitStack

F32 = mybir.dt.float32
BF16 = mybir.dt.bfloat16
FP16 = mybir.dt.float16
FP8 = mybir.dt.float8e4
U8 = mybir.dt.uint8
ALU = mybir.AluOpType
ACT = mybir.ActivationFunctionType
AX = mybir.AxisListType
RMAX = bass.bass_isa.ReduceOp.max

P = 128
N = 4096
D = 512
H = 8
HD = D // H
NT = N // P
FC = D // P
PAIRS = H // 2
BLK = 512
NB = N // BLK
TB = BLK // P
CH = 4
KC = NT // CH
CW = N // CH
EPS = 1e-5
HEADROOM0 = 60.0
NARROW = 9.0
MX_TOP = 32768.0
E_TOP = 16384.0
HEADROOM1 = 60.0
W_TOP = 64.0
EDGE = 2.0
EDGE_BYTE = 64
SB = 3
PB = 4
OWN = (4, 5, 11, 15, 19, 23, 27, 31)
SHARED = [k for k in range(N // P) if k not in OWN]
KB = 1024


def graph_layers(nc, x, adj, w0, a_dst, wk, wq, wv, wo, out):
    ctx = ExitStack()
    with ctx:
        def sb(name, shape, dt):
            return ctx.enter_context(nc.sbuf_tensor(name, shape, dt))

        def sem(name):
            return ctx.enter_context(nc.semaphore(name))

        adjt_dram = nc.dram_tensor("adjt_dram", [NT, P, N], U8, kind="Internal").ap()
        x1_dram = nc.dram_tensor("x1_dram", [N, D], F32, kind="Internal").ap()
        w_dram = nc.dram_tensor("w_dram", [4, P, 2 * FC * D], FP16, kind="Internal").ap()
        q_dram = nc.dram_tensor("q_dram", [NB, 2, H, HD, BLK], FP16, kind="Internal").ap()

        nodes = sb("nodes", [P, NT, D], F32)
        wide = sb("wide", [P, 96 * KB // 4], F32)
        work = sb("work", [P, 45568 // 4], F32)

        def part(region, at, nbytes, dt):
            return region[:, at // 4:(at + nbytes) // 4].bitcast(dt)

        hta = part(wide, 0, 4 * KB, F32).rearrange("p (b c n) -> p b c n", b=2, c=FC)
        ha = part(wide, 4 * KB, 8 * KB, F32).rearrange("p (b n) -> p b n", b=TB)
        w0_sb = part(wide, 12 * KB, 8 * KB, F32).rearrange("p (c n) -> p c n", c=FC)
        adst = part(wide, 20 * KB, 2 * KB, F32)
        prod = part(wide, 22 * KB, 4 * KB, F32).rearrange("p (b n) -> p b n", b=2)
        wf = part(wide, 28 * KB, 32 * KB, F32).rearrange("p (m n) -> p m n", m=4)
        wsplit = part(wide, 60 * KB, 32 * KB, FP16).rearrange("p (m s n) -> p m s n", m=4, s=2)
        emx = part(wide, 0, 96 * KB, BF16).rearrange("p (t s n) -> p t s n", t=NT, s=3)
        emx_pair = part(wide, 0, 96 * KB, FP16).rearrange("p (t s n) -> p t s n", t=NT, s=3)
        tall = part(work, 38 * KB, KB, F32).rearrange("p (t h) -> p t h", t=NT)
        expt = part(work, 39 * KB, KB, F32).rearrange("p (t h) -> p t h", t=NT)
        esplit = part(work, 40 * KB, 3 * KB // 2, BF16).rearrange("p (t s h) -> p t s h", t=NT, s=3)
        esplit_pair = part(work, 40 * KB, 3 * KB // 2, FP16).rearrange("p (t s h) -> p t s h", t=NT, s=3)
        erest = part(work, 42 * KB, KB, F32).rearrange("p (t h) -> p t h", t=NT)
        adjf = part(work, 0, 16 * KB, F32).rearrange("p (c n) -> p c n", c=CH)
        adjb = part(work, 16 * KB, 8 * KB, BF16).rearrange("p (c n) -> p c n", c=CH)
        adjt = part(work, 24 * KB, 8 * KB, FP8).rearrange("p (b n) -> p b n", b=2)
        adjt_bytes = part(work, 24 * KB, 8 * KB, U8).rearrange("p (b n) -> p b n", b=2)
        xt = part(work, 32 * KB, 4 * KB, F32).rearrange("p (b n) -> p b n", b=2)
        att0 = part(work, 36 * KB, 2 * KB, F32)
        wq_sb = part(work, 0, 8 * KB, FP16).rearrange("p (s c n) -> p s c n", s=2, c=FC)
        wk_sb = part(work, 8 * KB, 8 * KB, FP16).rearrange("p (s c n) -> p s c n", s=2, c=FC)
        wv_sb = part(work, 16 * KB, 8 * KB, FP16).rearrange("p (s c n) -> p s c n", s=2, c=FC)
        wo_sb = part(work, 24 * KB, 8 * KB, FP16).rearrange("p (s c n) -> p s c n", s=2, c=FC)
        hd = part(work, 32 * KB, 4 * KB, F32).rearrange("p (b n) -> p b n", b=2)
        keys = part(wide, 0, 64 * KB, FP16).rearrange("p (h n) -> p h n", h=H)
        htd = part(wide, 64 * KB, 16 * KB, FP16).rearrange("p (b s c n) -> p b s c n", b=2, s=2, c=FC)
        hi = part(wide, 80 * KB, 4 * KB, FP16).rearrange("p (b n) -> p b n", b=4)
        lo = part(wide, 84 * KB, 4 * KB, FP16).rearrange("p (b n) -> p b n", b=4)
        sq = part(wide, 88 * KB, 2 * KB, BF16).rearrange("p (b n) -> p b n", b=2)
        norm_max = part(wide, 90 * KB, 4 * NB * 8, F32)
        mask = part(wide, 64 * KB, 16 * KB, U8).rearrange("p (t k n) -> p t k n", t=TB, k=NT)
        qs = [part(wide, (92 - 4 * r) * KB, 4 * KB, FP16).rearrange("p (s h n) -> p s h n", s=2, h=2)
              for r in range(PAIRS)]
        prob = part(work, 0, PB * 4 * KB, F32).rearrange("p (b h n) -> p b h n", b=PB, h=2)
        pool_sum = part(work, 16 * KB, 4 * KB, F32).rearrange("p (h n) -> p h n", h=2)
        own_sum = part(work, 20 * KB, 4 * KB, F32).rearrange("p (h n) -> p h n", h=2)
        xo = part(work, 40 * KB, 4 * KB, F32).rearrange("p (b n) -> p b n", b=2)
        ot = part(work, 32 * KB, 8 * KB, F32).rearrange("p (r n) -> p r n", r=PAIRS)
        ot_pair = part(work, 32 * KB, 8 * KB, FP16).rearrange("p (r s n) -> p r s n", r=PAIRS, s=2)

        identf = sb("identf", [P, P], F32)
        identb = sb("identb", [P, P], BF16)
        headones = sb("headones", [P, P], BF16)
        onesf = sb("onesf", [P, P], F32)
        loops = sb("loops", [P, P], U8)
        diag = sb("diag", [P, 2, P], U8)
        stats = sb("stats", [P, TB, 6], F32)
        mv = sb("mv", [P, NT, 2], F32)
        mv1 = sb("mv1", [P, 2, 2], F32)
        mva = sb("mva", [P, TB, 2], F32)
        std = sb("std", [P, NT], F32)
        rstd = sb("rstd", [P, NT], F32)
        nmr = sb("nmr", [P, NT], F32)
        small = sb("small", [P, 60], F32)
        ext = sb("ext", [P, 2 * H + 1], F32)
        ext_all = sb("ext_all", [P, 2 * H + 1], F32)
        mabs = sb("mabs", [P, NT], F32)
        wide_range = sb("wide_range", [P, 1], mybir.dt.int32)
        eps_c, room_c = small[:, 0:1], small[:, 1:2]
        mx_scale, mx_over, t_range = small[:, 2:3], small[:, 3:4], small[:, 4:5]
        range8 = small[:, 10:18]
        den8, rden8 = small[:, 18:26], small[:, 26:34]
        wmax, wmax_all, wscale, out_over = small[:, 34:38], small[:, 48:52], small[:, 52:56], small[:, 56:57]
        nm2, nm2_all = small[:, 40:42], small[:, 42:44]
        s_prod, s_root, alpha, neg_shift = (small[:, k:k + 1] for k in (44, 45, 46, 47))

        bank = [ctx.enter_context(nc.psum_tensor(f"bank{i}", [P, BLK], F32)) for i in range(6, 8)]
        score = [ctx.enter_context(nc.psum_tensor(f"score{i}", [P, 2, BLK], F32)) for i in range(SB)]
        bank = [sc[:, e, :] for sc in score for e in range(2)] + [b[:, :] for b in bank]

        AHEAD = 2

        consts_ready, waits_passed = sem("consts_ready"), sem("waits_passed")
        zeroed = sem("zeroed")
        x_in = [sem(f"x_in{g}") for g in range(2 * AHEAD + 1)]
        w0_in, adst_in = sem("w0_in"), sem("adst_in")
        stats_done, aggr_done = sem("stats_done"), sem("aggr_done")
        std_done, rstd_done, nmr_done = sem("std_done"), sem("rstd_done"), sem("nmr_done")
        a_h, a_tr, a_ht, a_mm, a_mx = sem("a_h"), sem("a_tr"), sem("a_ht"), sem("a_mm"), sem("a_mx")
        mva_done = sem("mva_done")
        a_prod, a_t = sem("a_prod"), sem("a_t")
        a_mabs, b_seq, b_flag = sem("a_mabs"), sem("b_seq"), sem("b_flag")
        ext_done, ext_all_done = sem("ext_done"), sem("ext_all_done")
        tsub_done, exp_done = sem("tsub_done"), sem("exp_done")
        e_zero = sem("e_zero")
        e_hi, e_rest, e_mid, e_low = (sem(n) for n in ("e_hi", "e_rest", "e_mid", "e_low"))
        b_val, b_hi, b_rest, b_mid, b_low = (sem(n) for n in ("b_val", "b_hi", "b_rest", "b_mid", "b_low"))
        adj_in = [sem(f"adj_in{c}") for c in range(CH)]
        c_cast, c_tr, c_adjt, c_mm, c_acc = (sem(n) for n in ("c_cast", "c_tr", "c_adjt", "c_mm", "c_acc"))
        loops_ready, diag_made, diag_out = sem("loops_ready"), sem("diag_made"), [sem(f"diag_out{u}") for u in range(2)]
        xt_in = [sem(f"xt_in{u}") for u in range(2)]
        adjt_out = [sem(f"adjt_out{u}") for u in range(2)]
        c_den, c_rden, c_att, c_x1, c_stat, c_aggr = (sem(n) for n in ("c_den", "c_rden", "c_att", "c_x1", "c_stat", "c_aggr"))
        x1_out, c_mv = sem("x1_out"), sem("c_mv")
        wq_in, wk_in, wv_in, wo_in = (sem(n) for n in ("wq_in", "wk_in", "wv_in", "wo_in"))
        w_in, w_out = sem("w_in"), sem("w_out")
        w_abs, w_max, w_inv, w_scale, w_scaled, w_hi, w_lo = (sem(n) for n in ("w_abs", "w_max", "w_inv", "w_scale", "w_scaled", "w_hi", "w_lo"))
        d_ht_hi, d_alpha = sem("d_ht_hi"), sem("d_alpha")
        d_h, d_tr, d_ht, d_v, d_vout = (sem(n) for n in ("d_h", "d_tr", "d_ht", "d_v", "d_vout"))
        d_qk, d_hi, d_lo, d_sq, d_nrm, d_nmax = (sem(n) for n in ("d_qk", "d_hi", "d_lo", "d_sq", "d_nrm", "d_nmax"))
        hi_out = [sem(f"hi_out{b}") for b in range(4)]
        lo_out = [sem(f"lo_out{b}") for b in range(4)]
        d_nm2, d_nm2_all, d_sprod, d_root, d_shift = (sem(n) for n in ("d_nm2", "d_nm2_all", "d_sprod", "d_root", "d_shift"))
        q_in = [sem(f"q_in{r}") for r in range(PAIRS)]
        mask_in = [sem(f"mask_in{c}") for c in range(CH)]
        s_ready, s_exp, p_masked, pv_done, den_done = (sem(n) for n in ("s_ready", "s_exp", "p_masked", "pv_done", "den_done"))
        divided, ot_high = sem("divided"), sem("ot_high")
        pool_added, own_added, sums_joined = sem("pool_added"), sem("own_added"), sem("sums_joined")
        o_copied, rden_done, ot_done, wo_done, out_ready = (sem(n) for n in ("o_copied", "rden_done", "ot_done", "wo_done", "out_ready"))
        xo_in = [sem(f"xo_in{b}") for b in range(2)]
        out_stored = [sem(f"out_stored{b}") for b in range(2)]

        CONSTS = 8
        PRODUCTS = [(a, b, c) for c in range(FC) for a, b in ((0, 0), (0, 1), (1, 0))]
        STEPS = PAIRS * NT
        POOL_ADDS, OWN_ADDS = len(SHARED) - 1, len(OWN) - 1

        def added(kt):
            return max((OWN if kt in OWN else SHARED).index(kt), 1)

        JOIN, SUM_UP, INVERT, DIVIDE, HIGH, LOW = 1, 3, (6, 8, 10, 13), 14, 16, 17
        after = {20: 0, 23: 1, 26: 2, 29: 3}
        ring = []
        for k in range(STEPS):
            ring.append(("scores", k))
            if k in after:
                ring.append(("output", after[k]))
        assert len(ring) % SB == 0 and len(after) == TB

        def settled(engine):
            engine.sem_inc(waits_passed, 1)

        block = ctx.enter_context(nc.Block())

        @block.sync
        def _(sp):
            for b in range(4):
                sp.sem_inc(hi_out[b], 32)
                sp.sem_inc(lo_out[b], 32)
            for g in range(NB):
                sp.dma_start(nodes[:, g * TB:(g + 1) * TB, :],
                             x[g * BLK:(g + 1) * BLK, :].rearrange("(t p) d -> p t d", p=P)).then_inc(x_in[min(g, 2 * AHEAD)], 16)
                if g == 0:
                    for c in range(FC):
                        sp.dma_start(w0_sb[:, c, :].rearrange("p (h d) -> p h d", h=H),
                                     w0[:, c * P:(c + 1) * P, :].rearrange("h p d -> p h d")).then_inc(w0_in, 16)
                    sp.dma_start(adst, a_dst.rearrange("(o h) d -> o (h d)", o=1).broadcast_to([P, D])).then_inc(adst_in, 16)

            for m, w in enumerate((wq, wk, wv, wo)):
                for c in range(FC):
                    if m == 3:
                        sp.dma_start(wf[:, m, c * D:(c + 1) * D], wo[2 * c:2 * c + 2, :, :].rearrange("h d n -> (h d) n")).then_inc(w_in, 16)
                        continue
                    sp.dma_start(wf[:, m, c * D:(c + 1) * D].rearrange("p (h d) -> p h d", h=H),
                                 w[:, c * P:(c + 1) * P, :].rearrange("h p d -> p h d")).then_inc(w_in, 16)

            def load_adj(n, c):
                sp.wait_ge(c_cast, CH * n + c + 1)
                settled(sp)
                sp.dma_start(adjf[:, c, :], adj[bass.ds(n * P, P), c * CW:(c + 1) * CW]).then_inc(adj_in[c], 16)

            def load_x(t, u):
                sp.wait_ge(c_x1, t + 1)
                settled(sp)
                sp.dma_start(xt[:, u, :], x[bass.ds(t * P, P), :]).then_inc(xt_in[u], 16)

            for u in range(2):
                sp.sem_inc(adjt_out[u], 16)
                sp.sem_inc(diag_out[u], 16)

            def store_adjt(n, u):
                sp.wait_ge(c_adjt, CH + CH * (n + 1))
                settled(sp)
                sp.dma_start(adjt_dram[bass.ds(n, 1), :, :].rearrange("o p n -> (o p) n"), adjt_bytes[:, u, :]).then_inc(adjt_out[u], 16)

            def store_diag(n, u, i):
                sp.wait_ge(adjt_out[u], 16 * (i + 2))
                settled(sp)
                sp.wait_ge(diag_made, 2 + n + 1)
                settled(sp)
                sp.dma_start(adjt_dram[bass.ds(n, 1), :, bass.ds(n * P, P)].rearrange("o p n -> (o p) n"), diag[:, u, :]).then_inc(diag_out[u], 16)

            def store_x1(t):
                sp.wait_ge(c_x1, 2 + t + 1)
                settled(sp)
                sp.dma_start(x1_dram[bass.ds(t * P, P), :],
                             nodes[:, bass.ds(t, 1), :].rearrange("p o d -> p (o d)")).then_inc(x1_out, 16)

            for c in range(CH):
                load_adj(0, c)
            def store_split(m):
                sp.wait_ge(w_lo, m + 1)
                sp.dma_start(w_dram[m, :, :], wsplit[:, m, :, :].rearrange("p s n -> p (s n)")).then_inc(w_out, 16)

            store_split(0)
            store_split(1)
            for c in range(CH):
                load_adj(1, c)
            store_split(2)
            store_split(3)
            load_x(0, 0)
            store_adjt(0, 0)
            with sp.Fori(0, NT // 2 - 1) as i:
                for u in range(2):
                    t = 2 * i + u
                    load_x(t + 1, 1 - u)
                    for c in range(CH):
                        load_adj(t + 2, c)
                    store_adjt(t + 1, 1 - u)
                    store_diag(t, u, i)
                    store_x1(t)
            load_x(NT - 1, 1)
            store_adjt(NT - 1, 1)
            for u in range(2):
                store_diag(NT - 2 + u, u, NT // 2 - 1)
            store_x1(NT - 2)
            store_x1(NT - 1)

            def load_split(dst, m, s):
                sp.dma_start(dst.rearrange("p s c n -> p (s c n)"), w_dram[m, :, :]).then_inc(s, 16)

            sp.wait_ge(w_out, 16 * 4)
            sp.wait_ge(c_cast, CH + CH * NT)
            load_split(wq_sb, 0, wq_in)
            load_split(wk_sb, 1, wk_in)
            sp.wait_ge(c_tr, CH + CH * NT)
            load_split(wv_sb, 2, wv_in)
            sp.wait_ge(c_mm, 2 + NT)
            for u in range(2):
                sp.wait_ge(adjt_out[u], 16 * (NT // 2 + 1))
                sp.wait_ge(diag_out[u], 16 * (NT // 2 + 1))
            load_split(wo_sb, 3, wo_in)

            def store_qk(g, idx):
                b, pair = idx % 4, idx % PAIRS
                for what, done, credit, stored, half in ((hi, d_hi, 0, hi_out, 0), (lo, d_lo, 2, lo_out, 1)):
                    sp.wait_ge(done, credit + g * 8 + idx + 1)
                    settled(sp)
                    for e in range(2):
                        src = what[e * HD:(e + 1) * HD, b, :]
                        if idx < PAIRS:
                            dst = keys[half * HD:(half + 1) * HD, 2 * pair + e, bass.ds(g * BLK, BLK)]
                        else:
                            dst = q_dram[bass.ds(g, 1), half, 2 * pair + e, :, :].rearrange("o d n -> (o d) n")
                        sp.dma_start(dst, src).then_inc(stored[b], 16)

            def load_q(qb, r):
                sp.wait_ge(s_ready, STEPS * qb + NT * (r + 1))
                settled(sp)
                for half in range(2):
                    for s in range(2):
                        sp.dma_start(qs[r][half * HD:(half + 1) * HD, s, :, :],
                                     q_dram[bass.ds(qb, 1), s, 2 * r:2 * r + 2, :, :].rearrange("o h d n -> (o d) h n")
                                     ).then_inc(q_in[r], 16)

            def load_mask(qb, c):
                sp.wait_ge(p_masked, STEPS * qb + STEPS - NT + KC * (c + 1))
                settled(sp)
                sp.dma_start(mask[:, :, c * KC:(c + 1) * KC, :].rearrange("p t k n -> p t (k n)"),
                             adjt_dram[bass.ds(qb * TB, TB), :, c * CW:(c + 1) * CW].rearrange("t p n -> p t n")
                             ).then_inc(mask_in[c], 16)

            with sp.Fori(0, NB - 1) as g:
                for idx in range(8):
                    store_qk(g, idx)
            for b in range(4):
                sp.wait_ge(hi_out[b], 32 * 3)
                sp.wait_ge(lo_out[b], 32 * 3)
            load_q(0, 0)
            for idx in range(8):
                store_qk(NB - 1, idx)

            for c in range(CH - 1):
                load_mask(0, c)
            sp.wait_ge(d_nm2, 2)
            load_q(0, 1)
            for b in range(4):
                sp.wait_ge(hi_out[b], 32 * (2 * NB + 1))
                sp.wait_ge(lo_out[b], 32 * (2 * NB + 1))
            load_q(0, 2)
            load_q(0, 3)
            load_mask(0, CH - 1)

            def load_block(qb):
                load_q(qb, 0)
                load_q(qb, 1)
                load_q(qb, 2)
                for c in range(CH - 1):
                    load_mask(qb, c)
                load_q(qb, 3)
                load_mask(qb, CH - 1)

            def load_x1(qb, r):
                sp.wait_ge(out_stored[r % 2], 16 * (2 * qb + r // 2 + 1))
                settled(sp)
                sp.dma_start(xo[:, r % 2, :], x1_dram[bass.ds(qb * BLK + r * P, P), :]).then_inc(xo_in[r % 2], 16)

            def store_out(qb, r):
                sp.wait_ge(out_ready, TB * qb + r + 1)
                settled(sp)
                sp.dma_start(out[bass.ds(qb * BLK + r * P, P), :], xo[:, r % 2, :]).then_inc(out_stored[r % 2], 16)

            def finish_block(qb):
                load_x1(qb, 0)
                load_x1(qb, 1)
                store_out(qb, 0)
                load_x1(qb, 2)
                store_out(qb, 1)
                load_x1(qb, 3)
                store_out(qb, 2)
                store_out(qb, 3)

            for b in range(2):
                sp.sem_inc(out_stored[b], 16)
            with sp.Fori(1, NB) as qb:
                load_block(qb)
                finish_block(qb - 1)
            finish_block(NB - 1)
            for b in range(2):
                sp.wait_ge(out_stored[b], 16 * (2 * NB + 1))

        @block.gpsimd
        def _(pool):
            nc.gpsimd.memset(identf[:, :], 0.0).then_inc(zeroed, 1)
            nc.gpsimd.memset(identb[:, :], 0.0).then_inc(zeroed, 1)
            nc.gpsimd.memset(onesf[:, :], 1.0).then_inc(consts_ready, 1)
            nc.gpsimd.memset(eps_c, EPS).then_inc(consts_ready, 1)
            nc.gpsimd.memset(esplit[:, :, 2, :], 0.0).then_inc(e_zero, 1)
            pool.wait_ge(zeroed, 2)
            for m in (identf, identb):
                nc.gpsimd.affine_select(out=m[:, :], in_=m[:, :], compare_op=ALU.not_equal, fill=1.0, base=0,
                                        pattern=[[-1, P]], channel_multiplier=1).then_inc(consts_ready, 1)

            pool.wait_ge(w_abs, 4)
            nc.gpsimd.partition_all_reduce(wmax_all, wmax, P, RMAX).then_inc(w_max, 1)
            for m in range(4):
                pool.wait_ge(w_hi, m + 1)
                nc.gpsimd.tensor_tensor(wsplit[:, m, 1, :], wf[:, m, :], wsplit[:, m, 0, :], ALU.subtract).then_inc(w_lo, 1)

            pool.wait_ge(ext_done, 3)
            nc.gpsimd.partition_all_reduce(ext_all[:, :], ext[:, :], P, RMAX).then_inc(ext_all_done, 1)

            pool.sem_inc(d_sq, 4)
            with pool.Fori(0, NB) as g:
                for idx in range(8):
                    pool.wait_ge(d_hi, g * 8 + idx + 1)
                    pool.wait_ge(d_nrm, g * 8 + idx + 1)
                    nc.gpsimd.tensor_tensor(sq[:, idx % 2, :], hi[:, idx % 4, :], hi[:, idx % 4, :], ALU.mult).then_inc(d_sq, 1)
            pool.wait_ge(d_nm2, 2)
            nc.gpsimd.partition_all_reduce(nm2_all, nm2, P, RMAX).then_inc(d_nm2_all, 1)

            pool.sem_inc(pool_added, POOL_ADDS)
            with pool.Fori(0, NB) as qb:
                for r in range(PAIRS):
                    pair = PAIRS * qb + r
                    for n in range(1, len(SHARED)):
                        k = r * NT + SHARED[n]
                        pool.wait_ge(p_masked, STEPS * (qb + 1) + k + 1)
                        if n == 1:
                            pool.wait_ge(sums_joined, pair + 1)
                            nc.gpsimd.tensor_tensor(pool_sum, prob[:, (r * NT + SHARED[0]) % PB, :, :], prob[:, k % PB, :, :],
                                                    ALU.add).then_inc(pool_added, 1)
                        else:
                            pool.wait_ge(pool_added, POOL_ADDS * (pair + 1) + n - 1)
                            nc.gpsimd.tensor_tensor(pool_sum, pool_sum, prob[:, k % PB, :, :], ALU.add).then_inc(pool_added, 1)

        @block.scalar
        def _(act):
            act.wait_ge(consts_ready, CONSTS)
            act.sem_inc(a_mx, 2)

            def std_a(g):
                act.wait_ge(aggr_done, TB * (g + 1))
                settled(act)
                nc.scalar.activation(std[:, bass.ds(g * TB, TB)], mv[:, bass.ds(g * TB, TB), 1], ACT.Sqrt, bias=eps_c).then_inc(std_done, 1)

            def norm_a(g, j):
                t = g * TB + j
                if j == 0:
                    act.wait_ge(nmr_done, g + 1)
                act.wait_ge(a_tr, t + 1)
                nc.scalar.activation(ha[:, j, :], nodes[:, bass.ds(t, 1), :].rearrange("p o d -> p (o d)"), ACT.Relu,
                                     bias=nmr[:, bass.ds(t, 1)], scale=rstd[:, bass.ds(t, 1)]).then_inc(a_h, 1)

            def block_a(g, more_stats, more, weights=()):
                if more_stats:
                    std_a(g + AHEAD)
                for j in range(TB):
                    t = g * TB + j
                    if more:
                        norm_a(g + 1, j)
                    if weights:
                        m = weights[j // 2]
                        if j % 2 == 0:
                            act.wait_ge(w_scale, 1)
                            nc.scalar.activation(wf[:, m, :], wf[:, m, :], ACT.Copy, scale=wscale[:, m:m + 1]).then_inc(w_scaled, 1)
                        else:
                            act.wait_ge(w_scaled, m + 1)
                            nc.scalar.copy(wsplit[:, m, 0, :], wf[:, m, :]).then_inc(w_hi, 1)
                    act.wait_ge(a_mm, 2 + t + 1)
                    settled(act)
                    nc.scalar.copy(nodes[:, bass.ds(t, 1), :].rearrange("p o d -> p (o d)"), bank[2 + j % 2]).then_inc(a_mx, 1)

            for g in range(AHEAD):
                std_a(g)
                if g == 0:
                    for j in range(TB):
                        norm_a(0, j)
            with act.Fori(0, AHEAD + 2) as g:
                block_a(g, True, True)
            block_a(AHEAD + 2, True, True, (0, 1))
            block_a(AHEAD + 3, True, True, (2, 3))
            block_a(NB - 2, False, True)
            block_a(NB - 1, False, False)

            act.sem_inc(c_adjt, CH)

            def adjt_piece(n, u, c):
                act.wait_ge(c_tr, CH + CH * n + c + 1)
                settled(act)
                nc.scalar.activation(adjt[:, u, c * CW:(c + 1) * CW], bank[4 + c].bitcast(BF16), ACT.Copy,
                                     saturate=False).then_inc(c_adjt, 1)

            def adjt_tile(n, u, i):
                act.wait_ge(c_mm, n + 1)
                act.wait_ge(diag_made, n + 1)
                act.wait_ge(adjt_out[u], 16 * (i + 1))
                for c in range(CH):
                    adjt_piece(n, u, c)

            adjt_tile(0, 0, 0)

            act.wait_ge(tsub_done, 1)
            nc.scalar.activation(expt, tall, ACT.Exp, bias=room_c).then_inc(exp_done, 1)
            act.wait_ge(exp_done, 1)
            act.wait_ge(w_out, 16 * 4)
            act.wait_ge(b_flag, 1)
            is_wide = act.value_load(wide_range[0:1, 0:1], min_val=0, max_val=1)
            with act.If(is_wide > 0):
                nc.scalar.activation(esplit[:, :, 0, :], expt, ACT.Copy, scale=E_TOP).then_inc(e_hi, 1)
                act.wait_ge(e_rest, 1)
                nc.scalar.copy(esplit[:, :, 1, :], erest).then_inc(e_mid, 1)
                for g in range(NB + 1):
                    if g < NB:
                        act.wait_ge(b_val, g + 1)
                        nc.scalar.copy(emx[:, g * TB:(g + 1) * TB, 0, :], nodes[:, g * TB:(g + 1) * TB, :]).then_inc(b_hi, 1)
                    if g >= 1:
                        act.wait_ge(b_rest, g)
                        nc.scalar.copy(emx[:, (g - 1) * TB:g * TB, 1, :], nodes[:, (g - 1) * TB:g * TB, :]).then_inc(b_mid, 1)
            with act.Else():
                nc.scalar.activation(esplit_pair[:, :, 0, :], expt, ACT.Copy, scale=E_TOP).then_inc(e_hi, 1)
                for g in range(NB):
                    act.wait_ge(b_val, g + 1)
                    nc.scalar.copy(emx_pair[:, g * TB:(g + 1) * TB, 0, :], nodes[:, g * TB:(g + 1) * TB, :]).then_inc(b_hi, 1)

            with act.Fori(0, NT // 2 - 1) as i:
                adjt_tile(2 * i + 1, 1, i)
                adjt_tile(2 * i + 2, 0, i + 1)
            adjt_tile(NT - 1, 1, NT // 2 - 1)

            act.wait_ge(c_mv, NT)
            nc.scalar.activation(std[:, :], mv[:, :, 1], ACT.Sqrt, bias=eps_c).then_inc(std_done, 1)
            act.sem_inc(d_vout, 2)

            def norm_tile(t, j):
                act.wait_ge(d_tr, t + 1)
                nc.scalar.activation(hd[:, j % 2, :], nodes[:, bass.ds(t, 1), :].rearrange("p o d -> p (o d)"), ACT.Relu,
                                     bias=nmr[:, bass.ds(t, 1)], scale=rstd[:, bass.ds(t, 1)]).then_inc(d_h, 1)

            act.wait_ge(nmr_done, NB + 1)
            act.wait_ge(x1_out, 16 * NT)
            for j in range(TB):
                norm_tile(j, j)

            def project(g, last):
                for j in range(TB):
                    t = g * TB + j
                    if not last:
                        norm_tile(t + TB, j)
                    act.wait_ge(d_v, 2 + t + 1)
                    settled(act)
                    nc.scalar.copy(nodes[:, bass.ds(t, 1), :].rearrange("p o d -> p (o d)"), bank[2 + j % 2]).then_inc(d_vout, 1)
                for idx in range(8):
                    act.wait_ge(d_qk, 2 + g * 8 + idx + 1)
                    act.wait_ge(hi_out[idx % 4], 32 * (2 * g + idx // 4 + 1))
                    act.wait_ge(d_sq, g * 8 + idx + 1)
                    nc.scalar.copy(hi[:, idx % 4, :], bank[4 + idx % 2]).then_inc(d_hi, 1)

            with act.Fori(0, NB - 1) as g:
                project(g, False)
            project(NB - 1, True)
            act.wait_ge(d_sprod, 1)
            nc.scalar.activation(s_root, s_prod, ACT.Sqrt).then_inc(d_root, 1)

            act.wait_ge(d_shift, 1)
            act.sem_inc(o_copied, 1)

            def copy_attention(qb, r, first=False):
                if r == 0 and not first:
                    act.wait_ge(wo_done, TB * qb)
                act.wait_ge(pv_done, PB + STEPS * qb + (r + 1) * NT)
                nc.scalar.copy(ot[:, r, :], bank[6]).then_inc(o_copied, 1)

            def attention_high(qb, r):
                act.wait_ge(divided, PAIRS * qb + r + 1)
                nc.scalar.copy(ot_pair[:, r, 0, :], bank[7]).then_inc(ot_high, 1)

            def exps(qb, first):
                for at, (kind, k) in enumerate(ring):
                    if kind == "output":
                        continue
                    act.wait_ge(s_ready, STEPS * (qb + 1) + k + 1)
                    sc = score[at % SB][:, :, :]
                    nc.scalar.activation(sc, sc, ACT.Exp, bias=neg_shift, scale=alpha).then_inc(s_exp, 1)
                    if k % NT == 1 and k > NT:
                        copy_attention(qb, k // NT - 1, first)
                    elif k == 1 and not first:
                        copy_attention(qb - 1, PAIRS - 1)
                    if k % NT == HIGH and k > NT:
                        attention_high(qb, k // NT - 1)
                    elif k == HIGH and not first:
                        attention_high(qb - 1, PAIRS - 1)

            exps(0, True)
            with act.Fori(1, NB) as qb:
                exps(qb, False)
            copy_attention(NB - 1, PAIRS - 1)
            attention_high(NB - 1, PAIRS - 1)

        @block.vector
        def _(dve):
            for e in range(2):
                for f in range(2):
                    nc.vector.memset(headones[e * HD:(e + 1) * HD, f * HD:(f + 1) * HD], float(e == f)).then_inc(consts_ready, 1)
            dve.sem_inc(a_ht, 2)
            dve.sem_inc(c_cast, CH)
            dve.sem_inc(c_acc, 2)
            dve.sem_inc(c_x1, 2)
            dve.sem_inc(diag_made, 2)

            def stats_a(g):
                for j in range(TB):
                    t = g * TB + j
                    nc.vector.bn_stats(stats[:, j, :], nodes[:, bass.ds(t, 1), :].rearrange("p o d -> p (o d)")).then_inc(stats_done, 1)
                for j in range(TB):
                    t = g * TB + j
                    dve.wait_ge(stats_done, t + 1)
                    settled(dve)
                    nc.vector.bn_aggr(mva[:, j, :], stats[:, j, :]).then_inc(mva_done, 1)
                dve.wait_ge(mva_done, TB * (g + 1))
                nc.vector.tensor_copy(mv[:, bass.ds(g * TB, TB), :], mva[:, :, :]).then_inc(aggr_done, TB)

            def factors_a(g):
                cols = bass.ds(g * TB, TB)
                dve.wait_ge(std_done, g + 1)
                settled(dve)
                nc.vector.reciprocal(rstd[:, cols], std[:, cols]).then_inc(rstd_done, 1)
                dve.wait_ge(rstd_done, g + 1)
                settled(dve)
                nc.vector.scalar_tensor_tensor(out=nmr[:, cols], in0=mv[:, cols, 0], scalar=-1.0, in1=rstd[:, cols],
                                               op0=ALU.mult, op1=ALU.mult).then_inc(nmr_done, 1)

            def copy_ha(t, j):
                dve.wait_ge(a_tr, TB + t + 1)
                dve.wait_ge(a_mm, t + 1)
                nc.vector.tensor_copy(hta[:, j % 2, :, :], bank[j % 2].rearrange("p (c n) -> p c n", c=FC)).then_inc(a_ht, 1)

            def logits_a(t, j):
                dve.wait_ge(a_mx, 2 + t + 1)
                nc.vector.tensor_tensor(prod[:, j % 2, :], nodes[:, bass.ds(t, 1), :].rearrange("p o d -> p (o d)"),
                                        adst, ALU.mult).then_inc(a_prod, 1)
                nc.vector.tensor_reduce(mabs[:, bass.ds(t, 1)], nodes[:, bass.ds(t, 1), :].rearrange("p o d -> p (o d)"),
                                        AX.X, ALU.max, apply_absolute_value=True).then_inc(a_mabs, 1)
                dve.wait_ge(a_prod, t + 1)
                nc.vector.tensor_reduce(tall[:, bass.ds(t, 1), :].rearrange("p o h -> p (o h)"),
                                        prod[:, j % 2, :].rearrange("p (h d) -> p h d", h=H), AX.X, ALU.add).then_inc(a_t, 1)

            def block_a(g, more_stats, more, weights=()):
                if more_stats:
                    stats_a(g + AHEAD)
                for j in range(TB):
                    t = g * TB + j
                    if more or j < 2:
                        copy_ha(t + 2, j)
                    if j >= 2 and weights:
                        m = weights[j - 2]
                        nc.vector.tensor_reduce(wmax[:, m:m + 1], wf[:, m, :], AX.X, ALU.max,
                                                apply_absolute_value=True).then_inc(w_abs, 1)
                    logits_a(t, j)
                    if j == 0 and more_stats:
                        factors_a(g + AHEAD)

            def cast_tile(n):
                for c in range(CH):
                    dve.wait_ge(adj_in[c], 16 * (n + 1))
                    dve.wait_ge(c_tr, CH * n + c + 1)
                    nc.vector.tensor_scalar(adjb[:, c, :], adjf[:, c, :], 0.0, EDGE, ALU.is_gt, ALU.mult).then_inc(c_cast, 1)

            for g in range(AHEAD):
                dve.wait_ge(x_in[g], 16)
                stats_a(g)
                factors_a(g)
                if g == 0:
                    copy_ha(0, 0)
                    copy_ha(1, 1)
            dve.wait_ge(adst_in, 16)
            for g in range(AHEAD):
                dve.wait_ge(x_in[g + AHEAD], 16)
                block_a(g, True, True)
            dve.wait_ge(x_in[2 * AHEAD], 16 * (NB - 2 * AHEAD))
            dve.wait_ge(w_in, 16 * 4 * FC)
            block_a(AHEAD, True, True, (0, 1))
            block_a(AHEAD + 1, True, True, (2, 3))
            dve.wait_ge(w_max, 1)
            nc.vector.tensor_scalar(wmax_all, wmax_all, 1e-12, None, ALU.max).then_inc(w_inv, 1)
            dve.wait_ge(w_inv, 1)
            nc.vector.reciprocal(wscale, wmax_all).then_inc(w_inv, 1)
            dve.wait_ge(w_inv, 2)
            nc.vector.tensor_scalar(wscale, wscale, W_TOP, None, ALU.mult).then_inc(w_scale, 1)
            nc.vector.scalar_tensor_tensor(out=out_over, in0=wmax_all[:, 2:3], scalar=1.0 / (W_TOP * W_TOP),
                                           in1=wmax_all[:, 3:4], op0=ALU.mult, op1=ALU.mult).then_inc(w_inv, 1)
            with dve.Fori(AHEAD + 2, NB - AHEAD) as g:
                block_a(g, True, True)
            cast_tile(0)
            block_a(NB - 2, False, True)
            block_a(NB - 1, False, False)

            def norm_factors(n):
                dve.wait_ge(std_done, n)
                nc.vector.reciprocal(rstd[:, :], std[:, :]).then_inc(rstd_done, 1)
                dve.wait_ge(rstd_done, n)
                nc.vector.scalar_tensor_tensor(out=nmr[:, :], in0=mv[:, :, 0], scalar=-1.0, in1=rstd[:, :],
                                               op0=ALU.mult, op1=ALU.mult).then_inc(nmr_done, 1)

            dve.wait_ge(a_t, NT)
            dve.wait_ge(a_mabs, NT)
            t_by_head = tall.rearrange("p t h -> p h t")
            nc.vector.tensor_reduce(ext[:, 0:H], t_by_head, AX.X, ALU.max).then_inc(ext_done, 1)
            nc.vector.tensor_reduce(ext[:, H:2 * H], t_by_head, AX.X, ALU.min, negate=True).then_inc(ext_done, 1)
            nc.vector.tensor_reduce(ext[:, 2 * H:2 * H + 1], mabs[:, :], AX.X, ALU.max).then_inc(ext_done, 1)
            dve.wait_ge(ext_all_done, 1)
            nc.vector.tensor_tensor(tall, tall, ext_all[:, 0:H].rearrange("p (o h) -> p o h", o=1).broadcast_to([P, NT, H]),
                                    ALU.subtract).then_inc(b_seq, 1)
            nc.vector.tensor_tensor(range8, ext_all[:, 0:H], ext_all[:, H:2 * H], ALU.add).then_inc(b_seq, 1)
            dve.wait_ge(b_seq, 2)
            nc.vector.tensor_reduce(t_range, range8, AX.X, ALU.max).then_inc(b_seq, 1)
            dve.wait_ge(b_seq, 3)
            nc.vector.tensor_scalar(room_c, t_range, NARROW, HEADROOM0, ALU.is_gt, ALU.mult).then_inc(tsub_done, 1)
            nc.vector.tensor_scalar(wide_range[:, :], t_range, NARROW, None, ALU.is_gt).then_inc(b_flag, 1)
            nc.vector.tensor_scalar(mx_over, ext_all[:, 2 * H:2 * H + 1], 1e-24, 1.0 / MX_TOP, ALU.max, ALU.mult).then_inc(b_seq, 1)
            dve.wait_ge(b_seq, 4)
            nc.vector.reciprocal(mx_scale, mx_over).then_inc(b_seq, 1)
            dve.wait_ge(b_seq, 5)
            nc.vector.tensor_scalar(mx_over, mx_over, E_TOP, None, ALU.mult).then_inc(b_seq, 1)
            cast_tile(1)
            dve.wait_ge(exp_done, 1)

            def weigh(g):
                v = nodes[:, g * TB:(g + 1) * TB, :].rearrange("p t (h d) -> p (t h) d", h=H)
                e = expt[:, g * TB:(g + 1) * TB, :].rearrange("p t (h o) -> p (t h) o", o=1).broadcast_to([P, TB * H, HD])
                nc.vector.scalar_tensor_tensor(out=v, in0=v, scalar=mx_scale, in1=e, op0=ALU.mult, op1=ALU.mult).then_inc(b_val, 1)

            def rest(g, high, out, done):
                nc.vector.tensor_tensor(out, nodes[:, g * TB:(g + 1) * TB, :], high[:, g * TB:(g + 1) * TB, 0, :],
                                        ALU.subtract).then_inc(done, 1)

            dve.wait_ge(b_seq, 6)
            dve.wait_ge(w_out, 16 * 4)
            dve.wait_ge(b_flag, 1)
            is_wide = dve.value_load(wide_range[0:1, 0:1], min_val=0, max_val=1)
            with dve.If(is_wide > 0):
                dve.wait_ge(e_hi, 1)
                nc.vector.scalar_tensor_tensor(out=erest, in0=expt, scalar=E_TOP, in1=esplit[:, :, 0, :],
                                               op0=ALU.mult, op1=ALU.subtract).then_inc(e_rest, 1)
                for g in range(NB + 1):
                    if g == 1:
                        dve.wait_ge(e_mid, 1)
                        dve.wait_ge(e_zero, 1)
                        nc.vector.tensor_tensor(esplit[:, :, 2, :], erest, esplit[:, :, 1, :], ALU.subtract).then_inc(e_low, 1)
                    if g < NB:
                        weigh(g)
                        dve.wait_ge(b_hi, g + 1)
                        rest(g, emx, nodes[:, g * TB:(g + 1) * TB, :], b_rest)
                    if g >= 1:
                        dve.wait_ge(b_mid, g)
                        nc.vector.tensor_tensor(emx[:, (g - 1) * TB:g * TB, 2, :], nodes[:, (g - 1) * TB:g * TB, :],
                                                emx[:, (g - 1) * TB:g * TB, 1, :], ALU.subtract).then_inc(b_low, 1)
            with dve.Else():
                weigh(0)
                dve.wait_ge(e_hi, 1)
                nc.vector.scalar_tensor_tensor(out=esplit_pair[:, :, 1, :], in0=expt, scalar=E_TOP, in1=esplit_pair[:, :, 0, :],
                                               op0=ALU.mult, op1=ALU.subtract).then_inc(e_low, 1)
                for g in range(NB):
                    if g + 1 < NB:
                        weigh(g + 1)
                    dve.wait_ge(b_hi, g + 1)
                    rest(g, emx_pair, emx_pair[:, g * TB:(g + 1) * TB, 1, :], b_low)

            dve.wait_ge(consts_ready, CONSTS)
            nc.vector.tensor_scalar(loops[:, :], identf[:, :], float(EDGE_BYTE), None, ALU.mult).then_inc(loops_ready, 1)
            dve.wait_ge(loops_ready, 1)

            def finish_tile(t, u, i):
                dve.wait_ge(c_adjt, CH + CH * (t + 1))
                dve.wait_ge(diag_out[u], 16 * (i + 1))
                settled(dve)
                nc.vector.tensor_tensor(diag[:, u, :], adjt_bytes[:, u, bass.ds(t * P, P)], loops[:, :], ALU.max).then_inc(diag_made, 1)
                dve.wait_ge(c_mm, 2 + t + 1)
                nc.vector.tensor_reduce(den8, bank[2 + u][:, 0:3 * H].rearrange("p (s h) -> p h s", s=3), AX.X, ALU.add).then_inc(c_den, 1)
                dve.wait_ge(c_den, t + 1)
                nc.vector.reciprocal(rden8, den8).then_inc(c_rden, 1)
                dve.wait_ge(c_rden, 2 * t + 1)
                nc.vector.tensor_scalar(rden8, rden8, mx_over, None, ALU.mult).then_inc(c_rden, 1)
                dve.wait_ge(c_rden, 2 * t + 2)
                nc.vector.tensor_tensor(att0.rearrange("p (h d) -> p h d", h=H), bank[u].rearrange("p (h d) -> p h d", h=H),
                                        rden8.rearrange("p (h o) -> p h o", o=1).broadcast_to([P, H, HD]),
                                        ALU.mult).then_inc(c_acc, 1)
                dve.wait_ge(c_acc, 2 + t + 1)
                dve.wait_ge(xt_in[u], 16 * (i + 1))
                row = nodes[:, bass.ds(t, 1), :].rearrange("p o d -> p (o d)")
                nc.vector.tensor_tensor(row, att0, xt[:, u, :], ALU.add).then_inc(c_x1, 1)
                dve.wait_ge(c_x1, 2 + t + 1)
                settled(dve)
                nc.vector.bn_stats(stats[:, u, :], row).then_inc(c_stat, 1)
                dve.wait_ge(c_stat, t + 1)
                settled(dve)
                nc.vector.bn_aggr(mv1[:, u, :], stats[:, u, :]).then_inc(c_aggr, 1)
                dve.wait_ge(c_aggr, t + 1)
                nc.vector.tensor_copy(mv[:, bass.ds(t, 1), :].rearrange("p o d -> p (o d)"), mv1[:, u, :]).then_inc(c_mv, 1)

            with dve.Fori(0, NT // 2 - 1) as i:
                for u in range(2):
                    cast_tile(2 * i + u + 2)
                    finish_tile(2 * i + u, u, i)
            for u in range(2):
                finish_tile(NT - 2 + u, u, NT // 2 - 1)

            dve.sem_inc(d_ht, 2)
            dve.sem_inc(d_lo, 2)
            dve.sem_inc(d_nmax, 2)
            dve.sem_inc(p_masked, STEPS)

            def copy_ht(g, j, u):
                t = g * TB + j
                dve.wait_ge(d_tr, 2 + t + 1)
                ht = bank[j % 2].rearrange("p (c n) -> p c n", c=FC)
                nc.vector.tensor_copy(htd[:, u, 0, :, j * P:(j + 1) * P], ht).then_inc(d_ht_hi, 1)
                dve.wait_ge(d_ht_hi, t + 1)
                nc.vector.tensor_tensor(htd[:, u, 1, :, j * P:(j + 1) * P], ht, htd[:, u, 0, :, j * P:(j + 1) * P],
                                        ALU.subtract).then_inc(d_ht, 1)

            norm_factors(NB + 1)
            for j in range(TB):
                copy_ht(0, j, 0)

            def norms(g, idx):
                kind = 1 if idx < PAIRS else 0
                dve.wait_ge(d_nrm, 2 + g * 8 + idx + 1)
                nc.vector.tensor_reduce(norm_max[:, bass.ds(g * 8 + kind * PAIRS + idx % PAIRS, 1)],
                                        bank[6 + idx % 2], AX.X, ALU.max).then_inc(d_nmax, 1)

            def project(g, u, last):
                if not last:
                    for j in range(TB):
                        copy_ht(g + 1, j, 1 - u)
                for idx in range(8):
                    dve.wait_ge(d_hi, g * 8 + idx + 1)
                    dve.wait_ge(lo_out[idx % 4], 32 * (2 * g + idx // 4 + 1))
                    nc.vector.tensor_tensor(lo[:, idx % 4, :], bank[4 + idx % 2], hi[:, idx % 4, :], ALU.subtract).then_inc(d_lo, 1)
                    if idx >= 2:
                        norms(g, idx - 2)
                norms(g, 6)
                norms(g, 7)

            with dve.Fori(0, NB // 2 - 1) as i:
                project(2 * i, 0, False)
                project(2 * i + 1, 1, False)
            project(NB - 2, 0, False)
            project(NB - 1, 1, True)

            dve.wait_ge(d_nmax, 2 + 8 * NB)
            for kind in range(2):
                nc.vector.tensor_reduce(nm2[:, kind:kind + 1],
                                        norm_max.rearrange("p (g k r) -> p k g r", g=NB, k=2)[:, kind, :, :],
                                        AX.XY, ALU.max).then_inc(d_nm2, 1)
            dve.wait_ge(d_nm2_all, 1)
            nc.vector.tensor_tensor(s_prod, nm2_all[:, 0:1], nm2_all[:, 1:2], ALU.mult).then_inc(d_sprod, 1)
            nc.vector.scalar_tensor_tensor(out=alpha, in0=wmax_all[:, 0:1], scalar=1.0 / (HD ** 0.5 * W_TOP * W_TOP),
                                           in1=wmax_all[:, 1:2], op0=ALU.mult, op1=ALU.mult).then_inc(d_alpha, 1)
            dve.wait_ge(d_alpha, 1)
            dve.wait_ge(d_root, 1)
            nc.vector.scalar_tensor_tensor(out=neg_shift, in0=s_root, scalar=-1.0, in1=alpha, op0=ALU.mult, op1=ALU.mult).then_inc(d_alpha, 1)
            dve.wait_ge(d_alpha, 2)
            nc.vector.tensor_scalar(neg_shift, neg_shift, HEADROOM1, 0.0, ALU.add, ALU.min).then_inc(d_shift, 1)

            dve.sem_inc(ot_done, 1)
            dve.sem_inc(own_added, OWN_ADDS)
            dve.sem_inc(sums_joined, 1)

            def add_own(qb, r, kt):
                n, k, pair = OWN.index(kt), r * NT + kt, PAIRS * qb + r
                if n == 0:
                    return
                dve.wait_ge(p_masked, STEPS * (qb + 1) + k + 1)
                if n == 1:
                    dve.wait_ge(den_done, pair + 1)
                    nc.vector.tensor_tensor(own_sum, prob[:, (r * NT + OWN[0]) % PB, :, :], prob[:, k % PB, :, :],
                                            ALU.add).then_inc(own_added, 1)
                else:
                    dve.wait_ge(own_added, OWN_ADDS * (pair + 1) + n - 1)
                    nc.vector.tensor_tensor(own_sum, own_sum, prob[:, k % PB, :, :], ALU.add).then_inc(own_added, 1)

            def join(qb, r):
                dve.wait_ge(own_added, OWN_ADDS * (PAIRS * qb + r + 2))
                dve.wait_ge(pool_added, POOL_ADDS * (PAIRS * qb + r + 2))
                nc.vector.tensor_tensor(own_sum, own_sum, pool_sum, ALU.add).then_inc(sums_joined, 1)

            def invert(qb, r, j):
                if j == 0:
                    dve.wait_ge(den_done, 1 + PAIRS * qb + r + 1)
                part_of = bank[7][:, j * P:(j + 1) * P]
                nc.vector.reciprocal(part_of, part_of).then_inc(rden_done, 1)

            def divide(qb, r):
                dve.wait_ge(rden_done, TB * (PAIRS * qb + r + 1))
                dve.wait_ge(o_copied, 1 + PAIRS * qb + r + 1)
                nc.vector.tensor_tensor(bank[7], ot[:, r, :], bank[7], ALU.mult).then_inc(divided, 1)

            def attention_low(qb, r):
                dve.wait_ge(ot_high, PAIRS * qb + r + 1)
                nc.vector.tensor_tensor(ot_pair[:, r, 1, :], bank[7], ot_pair[:, r, 0, :], ALU.subtract).then_inc(ot_done, 1)

            def add_x1(qb, r, src):
                dve.wait_ge(wo_done, TB * qb + r + 1)
                dve.wait_ge(xo_in[r % 2], 16 * (2 * qb + r // 2 + 1))
                nc.vector.scalar_tensor_tensor(out=xo[:, r % 2, :], in0=src, scalar=out_over, in1=xo[:, r % 2, :],
                                               op0=ALU.mult, op1=ALU.add).then_inc(out_ready, 1)

            def masks(qb, first):
                for at, (kind, k) in enumerate(ring):
                    if kind == "output":
                        if not first:
                            add_x1(qb - 1, k, score[at % SB][:, 0, :])
                        continue
                    r, kt = k // NT, k % NT
                    if r == 0 and kt % KC == 0:
                        dve.wait_ge(mask_in[kt // KC], 16 * (qb + 1))
                    dve.wait_ge(s_exp, STEPS * qb + k + 1)
                    dve.wait_ge(pv_done, STEPS * qb + k + 1)
                    before, used = (k - PB) // NT, (k - PB) % NT
                    if used in OWN:
                        dve.wait_ge(own_added, OWN_ADDS * (PAIRS * qb + before + 1) + added(used))
                    else:
                        dve.wait_ge(pool_added, POOL_ADDS * (PAIRS * qb + before + 1) + added(used))
                    nc.vector.tensor_tensor(prob[:, k % PB, :, :].rearrange("p h (t n) -> p h t n", t=TB),
                                            score[at % SB][:, :, :].rearrange("p h (t n) -> p h t n", t=TB),
                                            mask[:, :, kt, :].unsqueeze(1).broadcast_to([P, 2, TB, P]), ALU.mult).then_inc(p_masked, 1)
                    if kt in OWN:
                        add_own(qb, r, kt)
                    if r or not first:
                        done = (qb, r - 1) if r else (qb - 1, PAIRS - 1)
                        if kt == JOIN:
                            join(*done)
                        if kt in INVERT:
                            invert(*done, INVERT.index(kt))
                        if kt == DIVIDE:
                            divide(*done)
                        if kt == LOW:
                            attention_low(*done)

            masks(0, True)
            with dve.Fori(1, NB) as qb:
                masks(qb, False)
            join(NB - 1, PAIRS - 1)
            for j in range(TB):
                invert(NB - 1, PAIRS - 1, j)
            divide(NB - 1, PAIRS - 1)
            attention_low(NB - 1, PAIRS - 1)
            for r in range(TB):
                add_x1(NB - 1, r, score[r % SB][:, 0, :])

        @block.tensor
        def _(pe):
            pe.wait_ge(consts_ready, CONSTS)
            pe.sem_inc(a_tr, TB)
            pe.sem_inc(a_mm, 2)
            pe.sem_inc(c_tr, CH)
            pe.sem_inc(c_mm, 2)
            pe.sem_inc(d_tr, 2)
            pe.sem_inc(d_v, 2)
            pe.sem_inc(d_qk, 2)
            pe.sem_inc(d_nrm, 2)
            pe.sem_inc(s_ready, STEPS)

            def transpose_a(t, j):
                pe.wait_ge(a_h, t + 1)
                pe.wait_ge(a_ht, t + 1)
                for c in range(FC):
                    last = nc.tensor.transpose(bank[j % 2][:, c * P:(c + 1) * P], ha[:, j % TB, c * P:(c + 1) * P], identf[:, :])
                last.then_inc(a_tr, 1)

            def block_a(g, more):
                for j in range(TB):
                    t = g * TB + j
                    if more or j < 2:
                        transpose_a(t + 2, j + 2)
                    pe.wait_ge(a_ht, 2 + t + 1)
                    pe.wait_ge(a_mx, t + 1)
                    for c in range(FC):
                        last = nc.tensor.matmul(bank[2 + j % 2], hta[:, j % 2, c, :], w0_sb[:, c, :], start=c == 0, stop=c == FC - 1)
                    last.then_inc(a_mm, 1)

            transpose_a(0, 0)
            transpose_a(1, 1)
            pe.wait_ge(w0_in, 16 * FC)
            with pe.Fori(0, NB - 1) as g:
                block_a(g, True)
            block_a(NB - 1, False)

            def transpose_adj(n, c):
                pe.wait_ge(c_cast, CH + CH * n + c + 1)
                pe.wait_ge(c_adjt, CH * n + c + 1)
                for k in range(KC):
                    last = nc.tensor.transpose(bank[4 + c].bitcast(BF16)[:, k * P:(k + 1) * P], adjb[:, c, k * P:(k + 1) * P], identb[:, :])
                last.then_inc(c_tr, 1)

            for c in range(CH):
                transpose_adj(0, c)
            pe.wait_ge(e_low, 1)
            pe.wait_ge(e_zero, 1)

            def attend(t, u, first_tile, last_tile, emx_parts, e_parts, parts):
                pe.wait_ge(c_acc, t + 1)
                for c in range(CH):
                    pe.wait_ge(c_adjt, CH + CH * t + c + 1)
                    settled(pe)
                    for k in range(c * KC, (c + 1) * KC):
                        first, last_k = k == 0, k == NT - 1
                        if first_tile and k % TB == 0:
                            pe.wait_ge(b_low, k // TB + 1)
                        w = adjt[:, u, k * P:(k + 1) * P]
                        for s in range(parts):
                            nc.tensor.matmul(bank[u], w, emx_parts[:, k, s, :], start=first and s == 0, stop=last_k and s == parts - 1)
                        last = nc.tensor.matmul(bank[2 + u][:, 0:3 * H], w, e_parts[:, k, :, :].rearrange("p s h -> p (s h)"),
                                                start=first, stop=last_k)
                    if c == CH - 1:
                        last.then_inc(c_mm, 1)
                    if not last_tile:
                        transpose_adj(t + 1, c)

            def attend_all(*how):
                for u in range(2):
                    attend(u, u, u == 0, False, *how)
                with pe.Fori(1, NT // 2 - 1) as i:
                    for u in range(2):
                        attend(2 * i + u, u, False, False, *how)
                attend(NT - 2, 0, False, False, *how)
                attend(NT - 1, 1, False, True, *how)

            pe.wait_ge(b_flag, 1)
            is_wide = pe.value_load(wide_range[0:1, 0:1], min_val=0, max_val=1)
            with pe.If(is_wide > 0):
                attend_all(emx, esplit, 3)
            with pe.Else():
                attend_all(emx_pair, esplit_pair, 2)

            def transpose_d(g, j):
                t = g * TB + j
                pe.wait_ge(d_h, t + 1)
                pe.wait_ge(d_ht, t + 1)
                for c in range(FC):
                    last = nc.tensor.transpose(bank[j % 2][:, c * P:(c + 1) * P], hd[:, j % 2, c * P:(c + 1) * P], identf[:, :])
                last.then_inc(d_tr, 1)

            def norm(g, idx):
                pe.wait_ge(d_sq, 4 + g * 8 + idx + 1)
                pe.wait_ge(d_nmax, g * 8 + idx + 1)
                nc.tensor.matmul(bank[6 + idx % 2], headones[:, :], sq[:, idx % 2, :], start=True, stop=True).then_inc(d_nrm, 1)

            def project(g, u, first_block, last_block):
                pe.wait_ge(d_ht, 2 + TB * (g + 1))
                for j in range(TB):
                    t = g * TB + j
                    pe.wait_ge(d_vout, t + 1)
                    for n, (hs, ws, c) in enumerate(PRODUCTS):
                        last = nc.tensor.matmul(bank[2 + j % 2], htd[:, u, hs, c, j * P:(j + 1) * P], wv_sb[:, ws, c, :],
                                                start=n == 0, stop=n == len(PRODUCTS) - 1)
                    last.then_inc(d_v, 1)
                    if not last_block:
                        transpose_d(g + 1, j)
                    if not first_block and j < 2:
                        norm(g - 1, 6 + j)
                for idx in range(8):
                    w = wk_sb if idx < PAIRS else wq_sb
                    pair = idx % PAIRS
                    pe.wait_ge(d_lo, g * 8 + idx + 1)
                    for n, (ws, hs, c) in enumerate(PRODUCTS):
                        last = nc.tensor.matmul(bank[4 + idx % 2], w[:, ws, c, pair * P:(pair + 1) * P], htd[:, u, hs, c, :],
                                                start=n == 0, stop=n == len(PRODUCTS) - 1)
                    last.then_inc(d_qk, 1)
                    if idx >= 2:
                        norm(g, idx - 2)
                if last_block:
                    norm(g, 6)
                    norm(g, 7)

            for j in range(TB):
                transpose_d(0, j)
            for s in (wv_in, wk_in, wq_in):
                pe.wait_ge(s, 16)
            project(0, 0, True, False)
            project(1, 1, False, False)
            with pe.Fori(1, NB // 2 - 1) as i:
                project(2 * i, 0, False, False)
                project(2 * i + 1, 1, False, False)
            project(NB - 2, 0, False, False)
            project(NB - 1, 1, False, True)

            pe.sem_inc(pv_done, PB)
            pe.sem_inc(den_done, 1)
            pe.wait_ge(d_vout, 2 + NT)
            pe.wait_ge(d_lo, 2 + 8 * NB)
            for b in range(PAIRS):
                pe.wait_ge(hi_out[b], 32 * 2 * NB)
                pe.wait_ge(lo_out[b], 32 * 2 * NB)
            pe.wait_ge(wo_in, 16)

            def scores(qb, k, buf):
                r, kt = k // NT, k % NT
                if kt == 0:
                    pe.wait_ge(q_in[r], 64 * (qb + 1))
                for e in range(2):
                    for s in range(2):
                        last = nc.tensor.matmul(score[buf][:, e, :], keys[:, 2 * r + e, kt * P:(kt + 1) * P],
                                                qs[r][:, s, e, :], start=s == 0, stop=s == 1)
                last.then_inc(s_ready, 1)

            def output(qb, r, buf):
                pe.wait_ge(ot_done, 1 + PAIRS * (qb + 1))
                for n, (os, ws, c) in enumerate(PRODUCTS):
                    last = nc.tensor.matmul(score[buf][:, 0, :], ot_pair[:, c, os, r * P:(r + 1) * P], wo_sb[:, ws, c, :],
                                            start=n == 0, stop=n == len(PRODUCTS) - 1)
                last.then_inc(wo_done, 1)

            def values(qb, k):
                r, kt = k // NT, k % NT
                if kt == 0:
                    pe.wait_ge(o_copied, PAIRS * qb + r + 1)
                pe.wait_ge(p_masked, STEPS * (qb + 1) + k + 1)
                for e in range(2):
                    last = nc.tensor.matmul(bank[6][e * HD:(e + 1) * HD, :],
                                            nodes[:, kt, (2 * r + e) * HD:(2 * r + e + 1) * HD],
                                            prob[:, k % PB, e, :], start=kt == 0, stop=kt == NT - 1)
                last.then_inc(pv_done, 1)

            def denominators(qb, r):
                pe.wait_ge(ot_done, PAIRS * qb + r + 1)
                pe.wait_ge(sums_joined, 1 + PAIRS * qb + r + 1)
                for e in range(2):
                    last = nc.tensor.matmul(bank[7][e * HD:(e + 1) * HD, :], onesf[:, 0:HD], own_sum[:, e, :], start=True, stop=True)
                last.then_inc(den_done, 1)

            def attention(qb, first):
                for at in range(len(ring)):
                    before, k = ring[at - SB]
                    if at < SB:
                        if not first:
                            values(qb - 1, k)
                    elif before == "scores":
                        values(qb, k)
                        if k % NT == SUM_UP and k > NT:
                            denominators(qb, k // NT - 1)
                        elif k == SUM_UP and not first:
                            denominators(qb - 1, PAIRS - 1)
                    elif not first:
                        pe.wait_ge(out_ready, TB * (qb - 1) + k + 1)
                    kind, k = ring[at]
                    if kind == "scores":
                        scores(qb, k, at % SB)
                    elif not first:
                        output(qb - 1, k, at % SB)

            attention(0, True)
            with pe.Fori(1, NB) as qb:
                attention(qb, False)
            for at in range(-SB, 0):
                values(NB - 1, ring[at][1])
            denominators(NB - 1, PAIRS - 1)
            for r in range(TB):
                if r >= SB:
                    pe.wait_ge(out_ready, TB * (NB - 1) + r - SB + 1)
                output(NB - 1, r, r % SB)


_INS = ["x", "adj", "L0_gnn_W", "L0_gnn_a_dst", "L1_gnn_Wks", "L1_gnn_Wqs", "L1_gnn_Wvs", "L1_gnn_Wo"]


def kernel(x, adj, L0_gnn_W, L0_gnn_a_origin, L0_gnn_a_dst, L1_gnn_Wks, L1_gnn_Wqs, L1_gnn_Wvs, L1_gnn_Wo):
    import numpy as _np
    import concourse.bacc as _bacc
    from concourse import mybir as _mybir
    from concourse.bass_utils import run_bass_kernel_spmd as _run

    given = dict(zip(_INS, (x, adj, L0_gnn_W, L0_gnn_a_dst, L1_gnn_Wks, L1_gnn_Wqs, L1_gnn_Wvs, L1_gnn_Wo)))
    nc = _bacc.Bacc("TRN2", target_bir_lowering=False, num_devices=1)
    arrays, args = {}, []
    for name in _INS:
        a = _np.ascontiguousarray(given[name])
        arrays[f"in_{name}_dram"] = a
        args.append(nc.dram_tensor(f"in_{name}_dram", a.shape, _mybir.dt.from_np(a.dtype), kind="ExternalInput").ap())
    out = nc.dram_tensor("out_0_dram", (N, D), F32, kind="ExternalOutput").ap()
    graph_layers(nc, *args, out)
    r = _run(nc, [arrays], core_ids=[0])
    return r.results[0]["out_0_dram"]
```
